# Optimizing a Trainium2 kernel written in Bass

```python
import numpy as np
import jax
import jax.numpy as jnp

def _softmax(x, axis=-1):
    return jax.nn.softmax(x, axis=axis)

def _gelu(x):
    return jax.nn.gelu(x, approximate=True)

def _silu(x):
    return jax.nn.silu(x)

def _sigmoid(x):
    return jax.nn.sigmoid(x)

def _layernorm(x, axis=-1, eps=1e-05):
    m = jnp.mean(x, axis=axis, keepdims=True)
    v = jnp.var(x, axis=axis, keepdims=True)
    return (x - m) / jnp.sqrt(v + eps)

def _scatter_add(tgt, idx, src, axis=0):
    return tgt.at[idx].add(src)

def _segment_sum(src, seg, n):
    return jax.ops.segment_sum(src, seg, n)
kernel_name = 'mk_prb_d1_jaxref_r8_866db7'

def setup_inputs(seed: int=0):
    np.random.seed(seed)
    _w = jnp.asarray

    def _L0_attn_setup():
        import jax, jax.numpy as jnp
        import numpy as np
        B, N, DIM, H, DH = (2, 256, 128, 16, 64)
        INNER = H * DH
        EPS = 1e-12
        MAX_LOG_SCALE = np.log(1.0 / 0.01)
        key = jax.random.key(seed)
        k1, k2, k3, k4 = jax.random.split(key, 4)
        x = jax.random.normal(k1, (B, N, DIM), dtype=jnp.float32)
        w_qkv = jax.random.normal(k2, (DIM, 3 * INNER), dtype=jnp.float32) * DIM ** (-0.5)
        w_out = jax.random.normal(k3, (INNER, DIM), dtype=jnp.float32) * INNER ** (-0.5)
        b_out = jax.random.normal(k4, (DIM,), dtype=jnp.float32) * 0.01
        logit_scale = jnp.full((H, 1, 1), jnp.log(10.0), dtype=jnp.float32)
        return {'x': x, 'w_qkv': w_qkv, 'w_out': w_out, 'b_out': b_out, 'logit_scale': logit_scale}
    _L0_attn_in = _L0_attn_setup()

    def _L0_ffn_setup():
        import jax, jax.numpy as jnp
        import numpy as np
        DIM = 128
        DEPTH = 6
        HEADS = 16
        DIM_HEAD = 64
        WINDOW = 32
        INNER = HEADS * DIM_HEAD
        DIM_INNER = int(DIM * 4 * 2 / 3)
        QK_SCALE = 8.0

        def shift_tokens(t):
            a, s = jnp.split(t, 2, -1)
            s = jnp.pad(s, ((0, 0), (1, 0), (0, 0)))[:, :-1]
            return jnp.concatenate([a, s], -1)

        def l2norm(t):
            return t / jnp.maximum(jnp.linalg.norm(t, axis=-1, keepdims=True), 1e-12)

        def rotate_half(x):
            x1, x2 = jnp.split(x, 2, -1)
            return jnp.concatenate([-x2, x1], -1)

        def rotary_tables(n):
            half = jnp.arange(0, DIM_HEAD, 2, dtype=jnp.float32)
            inv_freq = 1.0 / 10000.0 ** (half / DIM_HEAD)
            t = jnp.arange(n, dtype=jnp.float32)
            freqs = t[:, None] * inv_freq[None, :]
            freqs = jnp.concatenate([freqs, freqs], -1)
            base_scale = (half + 0.4 * DIM_HEAD) / (1.4 * DIM_HEAD)
            power = (t - n // 2) / (WINDOW // 2)
            scale = base_scale[None, :] ** power[:, None]
            scale = jnp.concatenate([scale, scale], -1)
            return (freqs, scale)

        def local_attention(q, k, v):
            b, h, n, d = q.shape
            w = WINDOW
            nw = n // w
            bq = q.reshape(b, h, nw, w, d)
            bk = k.reshape(b, h, nw, w, d)
            bv = v.reshape(b, h, nw, w, d)

            def look(t):
                p = jnp.pad(t, ((0, 0), (0, 0), (1, 0), (0, 0), (0, 0)))
                return jnp.concatenate([p[:, :, :nw], p[:, :, 1:]], axis=3)
            bk2, bv2 = (look(bk), look(bv))
            seq = jnp.arange(n).reshape(nw, w)
            seq_p = jnp.pad(seq, ((1, 0), (0, 0)), constant_values=-1)
            jt = jnp.concatenate([seq_p[:nw], seq_p[1:]], axis=1)
            it = seq[:, :, None]
            jb = jt[:, None, :]
            mask = (it < jb) | (it > jb + w) | (jb == -1)
            sim = jnp.einsum('bhwie,bhwje->bhwij', bq, bk2) * QK_SCALE
            sim = jnp.where(mask, -jnp.finfo(sim.dtype).max, sim)
            attn = jax.nn.softmax(sim, -1)
            out = jnp.einsum('bhwij,bhwje->bhwie', attn, bv2)
            return out.reshape(b, h, n, d)

        def attn_layer(x, Wqkv, qs, ksc, Wo):
            b, n, _ = x.shape
            qkv = x @ Wqkv
            q, k, v = jnp.split(qkv, 3, -1)
            sh = lambda t: t.reshape(b, n, HEADS, DIM_HEAD).transpose(0, 2, 1, 3)
            q, k, v = (sh(q), sh(k), sh(v))
            q = l2norm(q) * qs
            k = l2norm(k) * ksc
            freqs, scale = rotary_tables(n)
            cos, sin = (jnp.cos(freqs), jnp.sin(freqs))
            q = q * cos * scale + rotate_half(q) * sin * scale
            inv = 1.0 / scale
            k = k * cos * inv + rotate_half(k) * sin * inv
            out = local_attention(q, k, v)
            out = out.transpose(0, 2, 1, 3).reshape(b, n, INNER)
            return out @ Wo

        def ffn_layer(x, g, bln, W1, b1, W2, b2):
            mu = x.mean(-1, keepdims=True)
            var = ((x - mu) ** 2).mean(-1, keepdims=True)
            xn = (x - mu) / jnp.sqrt(var + 1e-05) * g + bln
            hg = xn @ W1 + b1
            a, gate = jnp.split(hg, 2, -1)
            return a * jax.nn.gelu(gate, approximate=False) @ W2 + b2
        key = jax.random.key(seed)
        ks = jax.random.split(key, 8)
        B, N = (2, 256)
        init = lambda k, shape: jax.random.normal(k, shape, jnp.float32) * 0.02
        return {'x': jax.random.normal(ks[0], (B, N, DIM), jnp.float32), 'Wqkv': init(ks[1], (DEPTH, DIM, 3 * INNER)), 'q_scale': jnp.ones((DEPTH, DIM_HEAD), jnp.float32), 'k_scale': jnp.ones((DEPTH, DIM_HEAD), jnp.float32), 'Wo': init(ks[2], (DEPTH, INNER, DIM)), 'ln_g': jnp.ones((DEPTH, DIM), jnp.float32), 'ln_b': jnp.zeros((DEPTH, DIM), jnp.float32), 'W1': init(ks[3], (DEPTH, DIM, 2 * DIM_INNER)), 'b1': jnp.zeros((DEPTH, 2 * DIM_INNER), jnp.float32), 'W2': init(ks[4], (DEPTH, DIM_INNER, DIM)), 'b2': jnp.zeros((DEPTH, DIM), jnp.float32)}
    _L0_ffn_in = _L0_ffn_setup()
    _d = {'L0_attn_x': _L0_attn_in['x'], 'L0_attn_w_qkv': _L0_attn_in['w_qkv'], 'L0_attn_w_out': _L0_attn_in['w_out'], 'L0_attn_b_out': _L0_attn_in['b_out'], 'L0_attn_logit_scale': _L0_attn_in['logit_scale'], 'L0_ffn_Wqkv': _L0_ffn_in['Wqkv'], 'L0_ffn_q_scale': _L0_ffn_in['q_scale'], 'L0_ffn_k_scale': _L0_ffn_in['k_scale'], 'L0_ffn_Wo': _L0_ffn_in['Wo'], 'L0_ffn_ln_g': _L0_ffn_in['ln_g'], 'L0_ffn_ln_b': _L0_ffn_in['ln_b'], 'L0_ffn_W1': _L0_ffn_in['W1'], 'L0_ffn_b1': _L0_ffn_in['b1'], 'L0_ffn_W2': _L0_ffn_in['W2'], 'L0_ffn_b2': _L0_ffn_in['b2']}
    _x0 = _d['L0_attn_x']
    _d['L0_attn_x'] = jax.random.normal(jax.random.fold_in(jax.random.key(seed), 1), (8, 512, 128), dtype=_x0.dtype)
    del _x0
    return _d

def reference(L0_attn_x, L0_attn_w_qkv, L0_attn_w_out, L0_attn_b_out, L0_attn_logit_scale, L0_ffn_Wqkv, L0_ffn_q_scale, L0_ffn_k_scale, L0_ffn_Wo, L0_ffn_ln_g, L0_ffn_ln_b, L0_ffn_W1, L0_ffn_b1, L0_ffn_W2, L0_ffn_b2):

    def _L0_attn_ref(x, w_qkv, w_out, b_out, logit_scale):
        import jax, jax.numpy as jnp
        import numpy as np
        B, N, DIM, H, DH = (2, 256, 128, 16, 64)
        INNER = H * DH
        EPS = 1e-12
        MAX_LOG_SCALE = np.log(1.0 / 0.01)
        b, n, dim = x.shape
        h = logit_scale.shape[0]
        qkv = x @ w_qkv
        q, k, v = jnp.split(qkv, 3, axis=-1)
        split_heads = lambda t: t.reshape(b, n, h, -1).transpose(0, 2, 1, 3)
        q, k, v = (split_heads(q), split_heads(k), split_heads(v))
        qn = q / jnp.maximum(jnp.linalg.norm(q, axis=-1, keepdims=True), EPS)
        kn = k / jnp.maximum(jnp.linalg.norm(k, axis=-1, keepdims=True), EPS)
        scale = jnp.exp(jnp.minimum(logit_scale, MAX_LOG_SCALE))
        cos_dots = jnp.einsum('bhid,bhjd->bhij', qn, kn) * scale
        attn = jax.nn.softmax(cos_dots, axis=-1)
        out = jnp.einsum('bhij,bhjd->bhid', attn, v)
        out = out.transpose(0, 2, 1, 3).reshape(b, n, -1)
        return out @ w_out + b_out

    def _L0_ffn_ref(x, Wqkv, q_scale, k_scale, Wo, ln_g, ln_b, W1, b1, W2, b2):
        import jax, jax.numpy as jnp
        import numpy as np
        DIM = 128
        DEPTH = 6
        HEADS = 16
        DIM_HEAD = 64
        WINDOW = 32
        INNER = HEADS * DIM_HEAD
        DIM_INNER = int(DIM * 4 * 2 / 3)
        QK_SCALE = 8.0

        def shift_tokens(t):
            a, s = jnp.split(t, 2, -1)
            s = jnp.pad(s, ((0, 0), (1, 0), (0, 0)))[:, :-1]
            return jnp.concatenate([a, s], -1)

        def l2norm(t):
            return t / jnp.maximum(jnp.linalg.norm(t, axis=-1, keepdims=True), 1e-12)

        def rotate_half(x):
            x1, x2 = jnp.split(x, 2, -1)
            return jnp.concatenate([-x2, x1], -1)

        def rotary_tables(n):
            half = jnp.arange(0, DIM_HEAD, 2, dtype=jnp.float32)
            inv_freq = 1.0 / 10000.0 ** (half / DIM_HEAD)
            t = jnp.arange(n, dtype=jnp.float32)
            freqs = t[:, None] * inv_freq[None, :]
            freqs = jnp.concatenate([freqs, freqs], -1)
            base_scale = (half + 0.4 * DIM_HEAD) / (1.4 * DIM_HEAD)
            power = (t - n // 2) / (WINDOW // 2)
            scale = base_scale[None, :] ** power[:, None]
            scale = jnp.concatenate([scale, scale], -1)
            return (freqs, scale)

        def local_attention(q, k, v):
            b, h, n, d = q.shape
            w = WINDOW
            nw = n // w
            bq = q.reshape(b, h, nw, w, d)
            bk = k.reshape(b, h, nw, w, d)
            bv = v.reshape(b, h, nw, w, d)

            def look(t):
                p = jnp.pad(t, ((0, 0), (0, 0), (1, 0), (0, 0), (0, 0)))
                return jnp.concatenate([p[:, :, :nw], p[:, :, 1:]], axis=3)
            bk2, bv2 = (look(bk), look(bv))
            seq = jnp.arange(n).reshape(nw, w)
            seq_p = jnp.pad(seq, ((1, 0), (0, 0)), constant_values=-1)
            jt = jnp.concatenate([seq_p[:nw], seq_p[1:]], axis=1)
            it = seq[:, :, None]
            jb = jt[:, None, :]
            mask = (it < jb) | (it > jb + w) | (jb == -1)
            sim = jnp.einsum('bhwie,bhwje->bhwij', bq, bk2) * QK_SCALE
            sim = jnp.where(mask, -jnp.finfo(sim.dtype).max, sim)
            attn = jax.nn.softmax(sim, -1)
            out = jnp.einsum('bhwij,bhwje->bhwie', attn, bv2)
            return out.reshape(b, h, n, d)

        def attn_layer(x, Wqkv, qs, ksc, Wo):
            b, n, _ = x.shape
            qkv = x @ Wqkv
            q, k, v = jnp.split(qkv, 3, -1)
            sh = lambda t: t.reshape(b, n, HEADS, DIM_HEAD).transpose(0, 2, 1, 3)
            q, k, v = (sh(q), sh(k), sh(v))
            q = l2norm(q) * qs
            k = l2norm(k) * ksc
            freqs, scale = rotary_tables(n)
            cos, sin = (jnp.cos(freqs), jnp.sin(freqs))
            q = q * cos * scale + rotate_half(q) * sin * scale
            inv = 1.0 / scale
            k = k * cos * inv + rotate_half(k) * sin * inv
            out = local_attention(q, k, v)
            out = out.transpose(0, 2, 1, 3).reshape(b, n, INNER)
            return out @ Wo

        def ffn_layer(x, g, bln, W1, b1, W2, b2):
            mu = x.mean(-1, keepdims=True)
            var = ((x - mu) ** 2).mean(-1, keepdims=True)
            xn = (x - mu) / jnp.sqrt(var + 1e-05) * g + bln
            hg = xn @ W1 + b1
            a, gate = jnp.split(hg, 2, -1)
            return a * jax.nn.gelu(gate, approximate=False) @ W2 + b2
        for i in range(DEPTH):
            x = attn_layer(shift_tokens(x), Wqkv[i], q_scale[i], k_scale[i], Wo[i]) + x
            x = ffn_layer(shift_tokens(x), ln_g[i], ln_b[i], W1[i], b1[i], W2[i], b2[i]) + x
        return x
    x = L0_attn_x
    xn = _layernorm(x, axis=-1)
    x = x + _L0_attn_ref(xn, L0_attn_w_qkv, L0_attn_w_out, L0_attn_b_out, L0_attn_logit_scale) + _L0_ffn_ref(xn, L0_ffn_Wqkv, L0_ffn_q_scale, L0_ffn_k_scale, L0_ffn_Wo, L0_ffn_ln_g, L0_ffn_ln_b, L0_ffn_W1, L0_ffn_b1, L0_ffn_W2, L0_ffn_b2)
    return x

_drawn_inputs = setup_inputs


def setup_inputs(seed=0):
    import zlib

    import numpy as np

    out = dict(_drawn_inputs(seed))
    spreads = {'L0_attn_logit_scale': (2.3025851249694824, 0.6),
     'L0_ffn_q_scale': (1.0, 0.6),
     'L0_ffn_k_scale': (1.0, 0.6),
     'L0_ffn_ln_g': (1.0, 0.6),
     'L0_ffn_ln_b': (0.0, 0.8),
     'L0_ffn_b1': (0.0, 0.8),
     'L0_ffn_b2': (0.0, 0.1)}
    factors = {'L0_attn_b_out': 33.835, 'L0_ffn_W1': 3.659, 'L0_ffn_W2': 3.594}
    for name, (base, spread) in spreads.items():
        noise = np.random.default_rng([zlib.crc32(name.encode()), seed]).standard_normal(out[name].shape)
        drawn = base * np.exp(spread * noise) if base else spread * noise
        out[name] = jnp.asarray(drawn.astype(out[name].dtype))
    for name, factor in factors.items():
        out[name] = (out[name] * factor).astype(out[name].dtype)
    return out
```

```python
from contextlib import ExitStack

import numpy as np
import concourse.bass as bass
from concourse import mybir

P = 128
ALU = mybir.AluOpType
ACT = mybir.ActivationFunctionType
F32 = mybir.dt.float32
I32 = mybir.dt.int32
BF16 = mybir.dt.bfloat16
X = mybir.AxisListType.X

DIM = 128
H, DH = 16, 64
PAIRS = H // 2
INNER = H * DH
WIN = 32
KEYS = 2 * WIN
SEQ = 512
NU = SEQ // P
NW = P // WIN
QK_SCALE = 8.0
MAX_LOG_SCALE = float(np.log(1.0 / 0.01))
NORM_FLOOR = 1e-24
EPS = 1e-5
FH = int(DIM * 4 * 2 / 3)
CH = [P, P, FH - 2 * P]
NC = len(CH)
ONES_ROW = 96
NEG = -1e30
RS = 11
RS_POOL = 12
TILES = H * NU


def build(nc, x_in, consts, a_logit, a_bout, a_wqk, a_wv, a_wo, l_wqk, l_wv, l_wo, l_scale, l_w1, l_w2, l_small, out):
    NB = x_in.shape[0]
    L = l_w1.shape[0]
    NBLK = NB * NU

    x_dram = x_in.rearrange("b (k p) d -> p (b k) d", p=P)
    out_dram = out.rearrange("b (k p) d -> b p k d", p=P)

    with ExitStack() as ctx:
        def sb(name, shape, dt=F32):
            return ctx.enter_context(nc.sbuf_tensor(name, shape, dt))

        credits = {}

        def sem(name, credit=0):
            s = ctx.enter_context(nc.semaphore(name))
            credits[name] = (s, credit)
            return s

        def at(name, n):
            return n + credits[name][1]

        x = sb("x", [P, NBLK * DIM])
        acc = sb("acc", [P, NBLK * DIM])
        xin = sb("xin", [P, 2, DIM])
        xsT = sb("xsT", [P, WIN + SEQ + 1])
        xdup = sb("xdup", [P, NW, 2, KEYS])
        xw = sb("xw", [P, NU, NW, DIM])
        qk = sb("qk", [P, 2 * INNER])
        sq = sb("sq", [P, 2 * INNER])
        t12 = sb("t12", [P, 4 * INNER])
        qn = sb("qn", [P, 2 * INNER])
        qT = sb("qT", [P, PAIRS, P])
        kpad = sb("kpad", [P, H, WIN + SEQ])
        es = sb("es", [P, INNER])
        pn = sb("pn", [P, INNER])
        pT = sb("pT", [P, PAIRS, P])
        y = sb("y", [P, H, P])
        wqk = sb("wqk", [P, 2 * INNER])
        wv = sb("wv", [P, PAIRS, DIM])
        wo = sb("wo", [P, PAIRS, DIM])
        mh = sb("mh", [P, H, DIM])
        cst = sb("cst", [P, P + 2 * KEYS])
        tab = sb("tab", [P, 2, NU, 2, DH])
        tabl = sb("tabl", [P, 2, NU, 2, DH])
        qks = sb("qks", [P, 2, DH])
        mask = sb("mask", [P, 2, H // 2, KEYS], BF16)
        identb = sb("identb", [P, P], BF16)
        onesd = sb("onesd", [P, P])
        ss = sb("ss", [P, 2 * H])
        c15 = sb("c15", [P, 2 * H])
        rn = sb("rn", [P, 2 * H])
        rt = sb("rt", [P, 2 * H])
        mx = sb("mx", [P, H])
        den = sb("den", [P, H])
        rden = sb("rden", [P, H])
        sc = sb("sc", [P, H])
        boutb = sb("boutb", [P, DIM])
        st = sb("st", [P, NU, 6])
        mv = sb("mv", [P, NU, 2])
        amx = sb("amx", [P, 4])
        anm = sb("anm", [P, 4])
        aden = sb("aden", [P, 4])
        ardn = sb("ardn", [P, 4])
        w1 = sb("w1", [P, 2 * FH])
        w1s = sb("w1s", [P, 2 * FH])
        w2 = sb("w2", [P, NC, DIM])
        sm = sb("sm", [P, 2 + 2 * NC])
        b1s = sb("b1s", [P, 2 * NC])
        fh = sb("fh", [P, NC, SEQ])

        ident = cst[:, 0:P]
        t1 = t12[:, 0:2 * INNER]
        t2 = t12[:, 2 * INNER:4 * INNER]
        kflat = kpad[:].rearrange("p h c -> p (h c)")
        qTA = kflat[:, 0:PAIRS * SEQ].rearrange("p (h c) -> p h c", h=PAIRS)
        kTA = kflat[:, PAIRS * SEQ:2 * PAIRS * SEQ].rearrange("p (h c) -> p h c", h=PAIRS)
        pTA = t12[:].rearrange("p (s k q) -> p s k q", s=2, k=NU)
        eA = es[:].rearrange("p (s k) -> p s k", s=2)
        yA = y[:].rearrange("p h c -> p (h c)")
        xnb = pn[:, 0:SEQ]
        xnT = xsT[:, WIN:WIN + SEQ]
        fin = qk[:, 0:SEQ]
        fT = qk[:, SEQ:2 * SEQ]
        fdg = qk[:, 2 * SEQ:3 * SEQ]
        fd = sq[:, 0:SEQ]
        fsq = sq[:, SEQ:2 * SEQ]
        fxn = sq[:, 2 * SEQ:3 * SEQ]
        fg = t12[:, 0:2 * SEQ].rearrange("p (s c) -> p s c", s=2)

        ps = ctx.enter_context(nc.psum_tensor("ps", [P, 8 * 512], F32))

        def bank(n, w=1):
            return ps[:, 512 * n:512 * (n + w)]

        pool0, pool1, pool2, pool3 = bank(0, 2), bank(2, 2), bank(4, 2), bank(6, 2)
        ps_out, ps_x = bank(6), bank(7)
        sbank = (0, 1, 7)

        s_ld = sem("s_ld")
        s_wa = sem("s_wa")
        s_wf = sem("s_wf")
        s_wqs = sem("s_wqs")
        s_avg = sem("s_avg")
        s_mask = sem("s_mask")
        s_row = sem("s_row")
        s_zero = sem("s_zero")
        s_sc = sem("s_sc")
        s_m = sem("s_m")
        s_msb = sem("s_msb")
        s_tab = sem("s_tab")
        s_rs = sem("s_rs")
        l_fl = sem("l_fl")
        l_gs = sem("l_gs")
        l_rs = sem("l_rs")
        a_st = sem("a_st")
        a_mv = sem("a_mv")
        a_xn = sem("a_xn")
        a_xcp = sem("a_xcp", 1)
        a_xt = sem("a_xt")
        a_xtsb = sem("a_xtsb")
        a_pj = sem("a_pj")
        a_qk = sem("a_qk", 1)
        a_sq = sem("a_sq")
        a_ss = sem("a_ss")
        a_qn = sem("a_qn", 1)
        a_t = sem("a_t", 1)
        a_tsb = sem("a_tsb", 1)
        a_s = sem("a_s")
        a_mx = sem("a_mx")
        a_nm = sem("a_nm")
        a_e = sem("a_e")
        a_rd = sem("a_rd")
        a_p = sem("a_p")
        a_pt = sem("a_pt")
        a_ptsb = sem("a_ptsb")
        a_y = sem("a_y")
        a_ysb = sem("a_ysb")
        a_o = sem("a_o")
        a_b = sem("a_b")
        a_acc = sem("a_acc", 1)
        l_xin = sem("l_xin")
        l_xt = sem("l_xt", 2)
        l_xsT = sem("l_xsT")
        l_xdup = sem("l_xdup")
        l_xw = sem("l_xw")
        l_xwsb = sem("l_xwsb", 1)
        l_pq = sem("l_pq")
        l_pk = sem("l_pk")
        l_q = sem("l_q")
        l_k = sem("l_k")
        l_sq = sem("l_sq", 1)
        l_ss = sem("l_ss", 1)
        l_rp = sem("l_rp", 2)
        l_rot = sem("l_rot")
        l_qn = sem("l_qn", 1)
        l_tq = sem("l_tq")
        l_tk = sem("l_tk", 1)
        l_qT = sem("l_qT")
        l_kT = sem("l_kT")
        l_kT2 = sem("l_kT2")
        l_s = sem("l_s", 1)
        l_mx = sem("l_mx")
        l_sub = sem("l_sub", 2)
        l_e = sem("l_e")
        l_den = sem("l_den")
        l_rd = sem("l_rd")
        l_p = sem("l_p", 1)
        l_pt = sem("l_pt", 1)
        l_pT = sem("l_pT")
        l_y0 = sem("l_y0")
        l_y1 = sem("l_y1")
        l_y0sb = sem("l_y0sb", 1)
        l_y1sb = sem("l_y1sb", 3)
        l_o = sem("l_o", 1)
        l_x = sem("l_x", 1)
        f_w = sem("f_w")
        f_b = sem("f_b")
        f_bs = sem("f_bs")
        f_in = sem("f_in")
        f_xt = sem("f_xt", 1)
        f_T = sem("f_T")
        f_mu = sem("f_mu")
        f_d = sem("f_d")
        f_sq = sem("f_sq")
        f_var = sem("f_var")
        f_dg = sem("f_dg")
        f_bc = sem("f_bc")
        f_xn = sem("f_xn", 1)
        f_u = sem("f_u", 1)
        f_g = sem("f_g")
        f_h = sem("f_h", 2)
        f_o = sem("f_o", 1)
        f_x = sem("f_x", 1)
        s_fin = sem("s_fin")
        s_out = sem("s_out")

        def keys(odd, u):
            rows = slice(odd * DH, (odd + 1) * DH)
            return (kpad[rows].rearrange("p (a s) c -> p a s c", s=2)[:, :, odd, WIN + u * P:WIN + (u + 1) * P],
                    pool1[rows].rearrange("p (h c) -> p h c", h=PAIRS))

        def layer_blocks(eng, l, turn):
            g0 = l * NBLK
            for c in (-3, -2, -1):
                turn(g0, 0, c, False)
            if NB > 1:
                with eng.Fori(0, NB - 1) as b:
                    for c in range(NU):
                        turn(g0 + b * NU, b * NU, c, False)
            for c in range(NU):
                turn(g0 + (NB - 1) * NU, (NB - 1) * NU, c, True)

        def stages(c, last):
            return [c + k >= 0 and (not last or c + k < NU) for k in range(4)]

        def slot(h):
            return h % 2 * PAIRS + h // 2

        def heads(ap, n):
            return ap.rearrange("p (h d) -> p h d", h=n)

        def rsqrt(src, dst, tmp, calls, pre, const):
            steps = [0]

            def link(ins):
                steps[0] += 1
                ins.then_inc(s_rs, 1)
                if steps[0] < RS:
                    nc.vector.wait_ge(s_rs, calls * RS + steps[0])

            link(nc.vector.tensor_scalar(src[1], src[0], const, None, pre))
            v = src[1]
            link(nc.vector.tensor_scalar(dst.bitcast(I32), v.bitcast(I32), -0.5, float(0x5F3759DF), ALU.mult, ALU.add))
            for _ in range(3):
                link(nc.vector.scalar_tensor_tensor(out=tmp, in0=dst, scalar=-0.5, in1=dst, op0=ALU.mult, op1=ALU.mult))
                link(nc.vector.tensor_tensor(tmp, tmp, v, ALU.mult))
                link(nc.vector.scalar_tensor_tensor(out=dst, in0=tmp, scalar=1.5, in1=dst, op0=ALU.add, op1=ALU.mult))

        block = ctx.enter_context(nc.Block())

        @block.sync
        def _(sp):
            for s, credit in credits.values():
                if credit:
                    sp.sem_inc(s, credit)
            sp.dma_start(cst[:], consts[:, 0:P + 2 * KEYS]).then_inc(s_ld, 16)
            sp.dma_start(sc[:], a_logit.partition_broadcast(P)).then_inc(s_ld, 16)
            sp.dma_start(boutb[:], a_bout.partition_broadcast(P)).then_inc(s_ld, 16)
            sp.dma_start(tab[:].rearrange("p a b c d -> p (a b c d)"), consts[:, P + 2 * KEYS:]).then_inc(s_ld, 16)
            for b in range(NB):
                sp.dma_start(acc[:, b * SEQ:(b + 1) * SEQ].rearrange("p (k d) -> p k d", k=NU),
                             x_dram[:, b * NU:(b + 1) * NU, :]).then_inc(s_ld, 16)

            def attention_weights(wqk_dram, wv_dram, wo_dram):
                sp.dma_start(wqk[:], wqk_dram).then_inc(s_wa, 16)
                sp.dma_start(wv[:].rearrange("p h d -> p (h d)"), wv_dram).then_inc(s_wa, 16)
                sp.dma_start(wo[:].rearrange("p h d -> p (h d)"), wo_dram).then_inc(s_wa, 16)

            def layer_row(ap, l):
                return ap[bass.ds(l, 1)].rearrange("a p n -> (a p) n")

            def layer_attention_weights(l):
                attention_weights(layer_row(l_wqk, l), layer_row(l_wv, l), layer_row(l_wo, l))

            def ffn_weights(l):
                sp.dma_start(w1[:], layer_row(l_w1, l)).then_inc(s_wf, 16)
                sp.dma_start(w2[:].rearrange("p c d -> p (c d)"), layer_row(l_w2, l)).then_inc(s_wf, 16)
                sp.dma_start(sm[:], layer_row(l_small, l)).then_inc(s_wf, 16)
                sp.dma_start(qks[:].rearrange("p a d -> p (a d)"),
                             l_scale[bass.ds(l, 1)].rearrange("a n -> (a n)").partition_broadcast(P)).then_inc(s_wqs, 16)

            attention_weights(a_wqk, a_wv, a_wo)
            ffn_weights(0)
            sp.wait_ge(a_pj, 2 * NBLK)
            sp.wait_ge(s_m, 1)
            layer_attention_weights(0)
            if L > 1:
                with sp.Fori(1, L) as l:
                    sp.wait_ge(l_pk, l * NBLK)
                    layer_attention_weights(l)
                    sp.wait_ge(f_x, at("f_x", l * NB))
                    ffn_weights(l)
            with sp.Fori(0, NB) as b:
                sp.wait_ge(s_fin, b + 1)
                sp.dma_start(out_dram[bass.ds(b, 1)].rearrange("b p k d -> p (b k) d"),
                             x[:, bass.ds(b * SEQ, SEQ)].rearrange("p (k d) -> p k d", k=NU)).then_inc(s_out, 16)
            sp.wait_ge(s_out, 16 * NB)

        @block.gpsimd
        def _(pool):
            nc.gpsimd.memset(onesd[:], 1.0 / DIM).then_inc(s_avg, 1)
            with pool.Fori(0, NB) as b:
                pool.wait_ge(a_xn, b + 1)
                nc.gpsimd.tensor_copy(x[:, bass.ds(b * SEQ, SEQ)], xnb).then_inc(a_xcp, 1)
            pool.wait_ge(a_acc, at("a_acc", NB))
            nc.gpsimd.memset(xsT[:], 0.0).then_inc(s_zero, 1)
            nc.gpsimd.memset(kpad[:], 0.0).then_inc(s_zero, 1)
            nc.gpsimd.memset(c15[:], 1.5).then_inc(s_zero, 1)
            pool.wait_ge(s_zero, 3)

            def turn(g, lb, c, last):
                has = stages(c, last)
                if has[2]:
                    n = c + 2
                    for i in range(2):
                        half = slice(i * INNER, (i + 1) * INNER)
                        pool.wait_ge(l_rp, at("l_rp", (g + n) * 2 + (i + 1)))
                        rotated = nc.gpsimd.tensor_tensor(t1[:, half], t1[:, half], t2[:, half], ALU.add)
                    rotated.then_inc(l_rot, 1)
                    pool.wait_ge(l_rot, g + (n + 1))
                    pool.wait_ge(l_gs, g + (n + 1))
                    done = (g + n) * RS_POOL
                    for step in range(RS_POOL):
                        out_, a, b, op = ((rt, rn, rn, ALU.mult), (rt, rt, ss, ALU.mult),
                                          (rt, c15, rt, ALU.subtract), (rn, rn, rt, ALU.mult))[step % 4]
                        if step:
                            pool.wait_ge(l_rs, done + step)
                        nc.gpsimd.tensor_tensor(out_[:], a[:], b[:], op).then_inc(l_rs, 1)
                if has[1]:
                    n = c + 1
                    pool.wait_ge(l_rd, g + (n + 1))
                    pool.wait_ge(l_pt, at("l_pt", g + n))
                    nc.gpsimd.tensor_tensor(heads(pn[:], H), heads(es[:], H),
                                            rden[:].unsqueeze(2).to_broadcast([P, H, KEYS]), ALU.mult).then_inc(l_p, 1)

            with pool.Fori(0, L) as l:
                layer_blocks(pool, l, turn)

        @block.scalar
        def _(act):
            act.wait_ge(s_ld, 16 * (4 + NB))
            act.activation(identb[:], ident, ACT.Copy).then_inc(s_mask, 1)
            for m in range(2):
                act.activation(mask[:, m], cst[:, P + m * KEYS:P + (m + 1) * KEYS].unsqueeze(1)
                               .to_broadcast([P, H // 2, KEYS]), ACT.Copy).then_inc(s_mask, 1)
            act.wait_ge(s_sc, 1)
            act.activation(sc[:], sc[:], ACT.Exp).then_inc(s_sc, 1)
            act.wait_ge(s_sc, 2)

            with act.Fori(0, NB) as b:
                act.wait_ge(a_xt, b + 1)
                act.activation(xnT, ps_x, ACT.Copy).then_inc(a_xtsb, 1)
                for u in range(NU):
                    g = b * NU + u
                    act.wait_ge(a_qn, at("a_qn", g))
                    for i in range(2):
                        act.wait_ge(a_pj, g * 2 + (i + 1))
                        act.activation(qk[:, i * INNER:(i + 1) * INNER], (pool0, pool1)[i], ACT.Copy).then_inc(a_qk, 1)
                    act.wait_ge(a_qk, at("a_qk", g * 2 + 2))
                    act.activation(sq[:], qk[:], ACT.Square).then_inc(a_sq, 1)
                    for i in range(2):
                        act.wait_ge(a_t, at("a_t", g * 2 + (i + 1)))
                        act.activation((qTA, kTA)[i][:, :, u * P:(u + 1) * P],
                                       (pool2, pool3)[i].rearrange("p (h c) -> p h c", h=PAIRS),
                                       ACT.Copy).then_inc(a_tsb, 1)
                for n in range(TILES + 2):
                    if n < TILES:
                        h = n // NU
                        act.wait_ge(a_nm, b * TILES + (n + 1))
                        if n >= 2:
                            act.wait_ge(a_pt, b * TILES + (n - 1))
                        act.activation(eA[:, n % 2], bank(sbank[n % 3]), ACT.Exp, bias=anm[:, n % 4:n % 4 + 1],
                                       scale=sc[:, h:h + 1], accum_out=aden[:, n % 4:n % 4 + 1]).then_inc(a_e, 1)
                    if 1 <= n <= TILES:
                        m = n - 1
                        h, qb = m // NU, m % NU
                        act.wait_ge(a_pt, b * TILES + (m + 1))
                        if h >= 2 and qb == 0:
                            act.wait_ge(a_y, b * H + (h - 1))
                        act.activation(pTA[:, h % 2, :, qb * P:(qb + 1) * P],
                                       bank(2 + m % 2).rearrange("p (k q) -> p k q", k=NU), ACT.Copy).then_inc(a_ptsb, 1)
                    if n >= NU + 1 and (n - 1) % NU == 0:
                        h = (n - 1) // NU - 1
                        act.wait_ge(a_y, b * H + (h + 1))
                        act.activation(yA[:, (h % 2) * SEQ:(h % 2 + 1) * SEQ], bank(4 + h % 2), ACT.Copy).then_inc(a_ysb, 1)

            def windows(u):
                a = xsT[:, u * P:u * P + KEYS]
                return bass.AP(a.tensor, a.offset, [list(a.ap[0]), [WIN, NW], [1, KEYS]])

            def copy_y(count, odd, done_y, copied, src):
                act.wait_ge(done_y, count)
                act.activation(y[:].rearrange("p (a s) (w q) -> p s w a q", s=2, w=NW)[:, odd],
                               src.rearrange("p (w a q) -> p w a q", w=NW, a=PAIRS), ACT.Copy).then_inc(copied, 1)

            def turn(g, lb, c, last):
                has = stages(c, last)
                if has[3]:
                    n = c + 3
                    act.wait_ge(l_xt, at("l_xt", g + (n - 1)))
                    act.activation(xin[:, n % 2], x[:, bass.ds((lb + n) * DIM, DIM)], ACT.Copy).then_inc(l_xin, 1)
                if has[2]:
                    n = c + 2
                    act.wait_ge(l_rp, at("l_rp", (g + n) * 2))
                    act.wait_ge(l_sq, at("l_sq", g + n))
                    act.wait_ge(l_pq, g + (n + 1))
                    act.activation(qk[:, 0:INNER], pool0, ACT.Copy).then_inc(l_q, 1)
                if has[2]:
                    n = c + 2
                    act.wait_ge(l_q, g + (n + 1))
                    act.wait_ge(l_ss, at("l_ss", g + n))
                    act.activation(sq[:, 0:INNER], qk[:, 0:INNER], ACT.Square)
                if has[2]:
                    n = c + 2
                    act.wait_ge(l_pk, g + (n + 1))
                    act.activation(qk[:, INNER:2 * INNER], pool1, ACT.Copy).then_inc(l_k, 1)
                if has[1]:
                    n = c + 1
                    act.wait_ge(l_tq, g + (n + 1))
                    act.activation(qT[:].rearrange("p h c -> p (h c)"), pool0, ACT.Copy).then_inc(l_qT, 1)
                if has[1]:
                    n = c + 1
                    u = n % NU
                    act.wait_ge(l_tk, at("l_tk", g + (n + 1)))
                    act.activation(*keys(0, u), ACT.Copy).then_inc(l_kT, 1)
                if has[0]:
                    n = c
                    act.wait_ge(l_pt, at("l_pt", g + (n + 1)))
                    act.activation(pT[:].rearrange("p h c -> p (h c)"), pool2, ACT.Copy).then_inc(l_pT, 1)
                if has[2]:
                    n = c + 2
                    act.wait_ge(l_xw, g + (n + 1))
                    act.activation(xw[:, n % NU].rearrange("p w d -> p (w d)"), ps_x, ACT.Copy).then_inc(l_xwsb, 1)
                if has[2]:
                    n = c + 2
                    act.wait_ge(l_k, g + (n + 1))
                    act.activation(sq[:, INNER:2 * INNER], qk[:, INNER:2 * INNER], ACT.Square).then_inc(l_sq, 1)
                if has[0]:
                    copy_y(g + (c + 1), 0, l_y0, l_y0sb, pool2)
                if has[3]:
                    n = c + 3
                    u = n % NU
                    act.wait_ge(l_xt, at("l_xt", g + (n + 1)))
                    act.activation(xsT[0:DH, WIN + u * P:WIN + (u + 1) * P], ps_x[0:DH, 0:P], ACT.Copy)
                    act.activation(xsT[DH:P, WIN + 1 + u * P:WIN + 1 + (u + 1) * P], ps_x[DH:P, 0:P],
                                   ACT.Copy).then_inc(l_xsT, 1)
                    act.wait_ge(l_xsT, g + (n + 1))
                    for twice in range(2):
                        dup = act.activation(xdup[:, :, twice, :], windows(u), ACT.Copy)
                    dup.then_inc(l_xdup, 1)
                if has[0]:
                    copy_y(g + (c + 1), 1, l_y1, l_y1sb, pool1)
                if has[1]:
                    n = c + 1
                    act.wait_ge(l_sub, at("l_sub", g + (n + 1)))
                    act.activation(es[:], es[:], ACT.Exp, scale=QK_SCALE).then_inc(l_e, 1)

            def ffn_in(n, b):
                act.wait_ge(f_xt, at("f_xt", n))
                act.activation(fin, x[:, bass.ds(b * SEQ, SEQ)], ACT.Copy).then_inc(f_in, 1)

            def ffn_copy(n):
                act.wait_ge(f_xt, at("f_xt", n + 1))
                act.activation(fT[0:DH, :], bank(0)[0:DH, :], ACT.Copy)
                act.activation(fT[DH:P, 1:SEQ], bank(0)[DH:P, 0:SEQ - 1], ACT.Copy).then_inc(f_T, 1)

            def ffn_square(n):
                act.wait_ge(f_d, n + 1)
                act.activation(fsq, fd, ACT.Square).then_inc(f_sq, 1)

            def ffn_gelu(n, c):
                act.wait_ge(f_u, at("f_u", n * NC + (c + 1)))
                act.wait_ge(f_h, at("f_h", n * NC + (c - 1)))
                act.activation(fg[0:CH[c], c % 2], bank((5, 7, 5)[c])[0:CH[c], :], ACT.Gelu,
                               bias=b1s[0:CH[c], NC + c:NC + c + 1]).then_inc(f_g, 1)

            act.wait_ge(s_zero, 2)
            act.wait_ge(a_xcp, at("a_xcp", NB))
            with act.Fori(0, L) as l:
                act.wait_ge(f_x, at("f_x", l * NB))
                layer_blocks(act, l, turn)
                act.wait_ge(l_x, at("l_x", (l + 1) * NBLK))
                ffn_in(l * NB, 0)
                act.wait_ge(f_xt, at("f_xt", l * NB + 1))
                act.activation(fT[DH:P, 0:1], xsT[DH:P, 0:1], ACT.Copy)
                ffn_copy(l * NB)
                if NB > 1:
                    ffn_in(l * NB + 1, 1)
                ffn_square(l * NB)
                act.wait_ge(f_bs, l + 1)

                def ffn_turn(n, b, more, further):
                    if more:
                        ffn_copy(n + 1)
                    ffn_gelu(n, 0)
                    if more:
                        ffn_square(n + 1)
                    ffn_gelu(n, 1)
                    if further:
                        ffn_in(n + 2, b + 2)
                    ffn_gelu(n, 2)

                if NB > 2:
                    with act.Fori(0, NB - 2) as b:
                        ffn_turn(l * NB + b, b, True, True)
                if NB > 1:
                    ffn_turn(l * NB + (NB - 2), NB - 2, True, False)
                ffn_turn(l * NB + (NB - 1), NB - 1, False, False)

        @block.vector
        def _(dve):
            def fold(n):
                dve.wait_ge(s_m, n + 1)
                nc.vector.tensor_copy(mh[:].rearrange("p h d -> p (h d)"), bank(2, 4)).then_inc(s_msb, 1)

            dve.wait_ge(s_ld, 16 * (4 + NB))
            nc.vector.tensor_scalar(sc[:], sc[:], MAX_LOG_SCALE, None, ALU.min).then_inc(s_sc, 1)
            nc.vector.memset(fh[DH:P, NC - 1], 0.0).then_inc(s_row, 1)
            dve.wait_ge(s_row, 1)
            nc.vector.memset(fh[ONES_ROW:ONES_ROW + 1, NC - 1], 1.0).then_inc(s_row, 1)
            fold(0)
            dve.wait_ge(s_sc, 2)

            with dve.Fori(0, NB) as b:
                tokens = acc[:, bass.ds(b * SEQ, SEQ)]
                for u in range(NU):
                    stat = nc.vector.bn_stats(st[:, u], acc[:, bass.ds(b * SEQ + u * P, P)])
                stat.then_inc(a_st, 1)
                dve.wait_ge(a_st, b + 1)
                nc.vector.memset(rt[:, 0:NU], 0.0)
                for u in range(NU):
                    stat = nc.vector.bn_aggr(mv[:, u], st[:, u])
                stat.then_inc(a_mv, 1)
                dve.wait_ge(a_mv, b + 1)
                rsqrt((mv[:, :, 1], ss[:, 0:NU]), rn[:, 0:NU], rt[:, 0:NU], b * (NU + 1), ALU.add, EPS)
                dve.wait_ge(s_rs, (b * (NU + 1) + 1) * RS)
                dve.wait_ge(a_xcp, at("a_xcp", b))
                for u in range(NU):
                    norm = nc.vector.tensor_scalar(xnb[:, u * P:(u + 1) * P], acc[:, bass.ds(b * SEQ + u * P, P)],
                                                   mv[:, u, 0:1], rn[:, u:u + 1], ALU.subtract, ALU.mult)
                norm.then_inc(a_xn, 1)
                for u in range(NU):
                    g = b * NU + u
                    dve.wait_ge(a_sq, g + 1)
                    nc.vector.tensor_reduce(ss[:], heads(sq[:], 2 * H), X, ALU.add).then_inc(a_ss, 1)
                    dve.wait_ge(a_ss, g + 1)
                    rsqrt((ss[:], ss[:]), rn[:], rt[:], b * (NU + 1) + (u + 1), ALU.max, NORM_FLOOR)
                    dve.wait_ge(s_rs, (b * (NU + 1) + (u + 2)) * RS)
                    dve.wait_ge(a_t, at("a_t", g * 2))
                    nc.vector.tensor_tensor(heads(qn[:], 2 * H), heads(qk[:], 2 * H),
                                            rn[:].unsqueeze(2).to_broadcast([P, 2 * H, DH]), ALU.mult).then_inc(a_qn, 1)
                for n in range(TILES + 1):
                    if n < TILES:
                        h, i = n // NU, n % 4
                        dve.wait_ge(a_s, b * TILES + (n + 1))
                        nc.vector.tensor_reduce(amx[:, i:i + 1], bank(sbank[n % 3]), X, ALU.max).then_inc(a_mx, 1)
                        dve.wait_ge(a_mx, b * TILES + (n + 1))
                        nc.vector.tensor_scalar(anm[:, i:i + 1], amx[:, i:i + 1], sc[:, h:h + 1], -1.0,
                                                ALU.mult, ALU.mult).then_inc(a_nm, 1)
                    if n >= 1:
                        m, i = n - 1, (n - 1) % 4
                        dve.wait_ge(a_e, b * TILES + (m + 1))
                        nc.vector.reciprocal(ardn[:, i:i + 1], aden[:, i:i + 1]).then_inc(a_rd, 1)
                        dve.wait_ge(a_rd, b * TILES + (m + 1))
                        nc.vector.tensor_scalar(eA[:, m % 2], eA[:, m % 2], ardn[:, i:i + 1], None, ALU.mult).then_inc(a_p, 1)
                tokens_b = tokens.rearrange("p (k d) -> p k d", k=NU)
                nc.vector.tensor_tensor(tokens_b, tokens_b, boutb[:].unsqueeze(1).to_broadcast([P, NU, DIM]),
                                        ALU.add).then_inc(a_b, 1)
                dve.wait_ge(a_b, b + 1)
                dve.wait_ge(a_o, b + 1)
                nc.vector.tensor_tensor(tokens, tokens, ps_out, ALU.add).then_inc(a_acc, 1)

            FIRST = NB * (NU + 1)

            def scale_tables(l):
                dve.wait_ge(s_wqs, (l + 1) * 16)
                nc.vector.tensor_tensor(tabl[:, 0].rearrange("p b c d -> p b (c d)"), tab[:, 0].rearrange("p b c d -> p b (c d)"),
                                        qks[:].rearrange("p c d -> p (c d)").unsqueeze(1).to_broadcast([P, NU, 2 * DH]),
                                        ALU.mult)
                for lo, hi in ((0, DH // 2), (DH // 2, 0)):
                    t = nc.vector.tensor_tensor(tabl[:, 1, :, :, lo:lo + DH // 2], tab[:, 1, :, :, lo:lo + DH // 2],
                                                qks[:, :, hi:hi + DH // 2].unsqueeze(1).to_broadcast([P, NU, 2, DH // 2]),
                                                ALU.mult)
                t.then_inc(s_tab, 1)
                dve.wait_ge(s_tab, l + 1)

            def turn(g, lb, c, last):
                has = stages(c, last)

                def odd_keys(n):
                    dve.wait_ge(l_tk, at("l_tk", g + (n + 1)))
                    nc.vector.tensor_copy(*keys(1, n % NU)).then_inc(l_kT2, 1)

                if has[1] and not has[2]:
                    odd_keys(c + 1)
                if has[2]:
                    n = c + 2
                    u = n % NU
                    for i, copied in enumerate((l_q, l_k)):
                        if i == 1 and has[1]:
                            odd_keys(c + 1)
                        half = slice(i * INNER, (i + 1) * INNER)
                        q3, t13, t23 = (heads(a[:, half], H) for a in (qk, t1, t2))
                        dve.wait_ge(copied, g + (n + 1))
                        if i == 0:
                            dve.wait_ge(l_qn, at("l_qn", g + n))
                        nc.vector.tensor_tensor(t13, q3, tabl[:, 0, u, i].unsqueeze(1).to_broadcast([P, H, DH]), ALU.mult)
                        for lo, hi in ((0, DH // 2), (DH // 2, 0)):
                            sine = nc.vector.tensor_tensor(
                                t23[:, :, lo:lo + DH // 2], q3[:, :, hi:hi + DH // 2],
                                tabl[:, 1, u, i, lo:lo + DH // 2].unsqueeze(1).to_broadcast([P, H, DH // 2]), ALU.mult)
                        sine.then_inc(l_rp, 1)
                    dve.wait_ge(l_sq, at("l_sq", g + (n + 1)))
                    nc.vector.tensor_reduce(ss[:], heads(sq[:], 2 * H), X, ALU.add).then_inc(l_ss, 1)
                    dve.wait_ge(l_ss, at("l_ss", g + (n + 1)))
                    nc.vector.tensor_scalar(ss[:], ss[:], NORM_FLOOR, 0.5, ALU.max, ALU.mult).then_inc(l_fl, 1)
                    dve.wait_ge(l_fl, g + (n + 1))
                    nc.vector.tensor_scalar(rn[:].bitcast(I32), ss[:].bitcast(I32), -0.5, float(0x5F3759DF - (1 << 22)),
                                            ALU.mult, ALU.add).then_inc(l_gs, 1)
                if has[1]:
                    n = c + 1
                    dve.wait_ge(l_s, at("l_s", g + (n + 1)))
                    nc.vector.tensor_reduce(mx[:], heads(pool0, H), X, ALU.max).then_inc(l_mx, 1)
                    dve.wait_ge(l_mx, g + (n + 1))
                    dve.wait_ge(l_p, at("l_p", g + n))
                    nc.vector.tensor_tensor(heads(es[:], H), heads(pool0, H),
                                            mx[:].unsqueeze(2).to_broadcast([P, H, KEYS]), ALU.subtract).then_inc(l_sub, 1)
                if has[1]:
                    n = c + 1
                    dve.wait_ge(l_e, g + (n + 1))
                    nc.vector.tensor_reduce(den[:], heads(es[:], H), X, ALU.add).then_inc(l_den, 1)
                    dve.wait_ge(l_den, g + (n + 1))
                    nc.vector.reciprocal(rden[:], den[:]).then_inc(l_rd, 1)
                if has[0]:
                    n = c
                    dve.wait_ge(l_o, at("l_o", g + (n + 1)))
                    xb = x[:, bass.ds((lb + n) * DIM, DIM)]
                    nc.vector.tensor_tensor(xb, xb, ps_out[:, 0:DIM], ALU.add).then_inc(l_x, 1)
                if has[2]:
                    n = c + 2
                    dve.wait_ge(l_rs, (g + (n + 1)) * RS_POOL)
                    dve.wait_ge(l_tk, at("l_tk", g + n))
                    nc.vector.tensor_tensor(heads(qn[:], 2 * H), heads(t1, 2 * H),
                                            rn[:].unsqueeze(2).to_broadcast([P, 2 * H, DH]), ALU.mult).then_inc(l_qn, 1)

            def ffn_bias(l):
                dve.wait_ge(s_wf, (l + 1) * 48)
                nc.vector.tensor_scalar(w1s[:], w1[:], sm[:, 0:1], None, ALU.mult).then_inc(f_w, 1)
                dve.wait_ge(f_b, l + 1)
                for half in range(2):
                    c0 = half * NC
                    nc.vector.tensor_tensor(b1s[:, c0:c0 + NC - 1], sm[:, 2 + c0:1 + c0 + NC], bank(1)[:, c0:c0 + NC - 1], ALU.add)
                    last = nc.vector.tensor_tensor(b1s[0:CH[-1], c0 + NC - 1:c0 + NC], sm[0:CH[-1], 1 + c0 + NC:2 + c0 + NC],
                                                   bank(1)[0:CH[-1], c0 + NC - 1:c0 + NC], ALU.add)
                last.then_inc(f_bs, 1)
                dve.wait_ge(f_bs, l + 1)

            def ffn_deviation(n):
                dve.wait_ge(f_mu, n + 1)
                dve.wait_ge(f_xn, at("f_xn", n))
                nc.vector.tensor_tensor(fd, fT, bank(1), ALU.subtract).then_inc(f_d, 1)

            def ffn_rstd(n):
                dve.wait_ge(f_var, n + 1)
                rsqrt((bank(2)[:, 0:NU], ss[:, 0:NU]), rn[:, 0:NU], rt[:, 0:NU], n + FIRST, ALU.add, EPS)
                dve.wait_ge(s_rs, (n + (FIRST + 1)) * RS)
                for k in range(NU):
                    dg = nc.vector.tensor_scalar(fdg[:, k * P:(k + 1) * P], ident, rn[:, k:k + 1], float(DIM),
                                                 ALU.mult, ALU.mult)
                dg.then_inc(f_dg, 1)

            def ffn_norm(n):
                dve.wait_ge(f_bc, n + 1)
                dve.wait_ge(f_u, at("f_u", n * NC))
                nc.vector.tensor_tensor(fxn, fd, bank(3), ALU.mult).then_inc(f_xn, 1)

            def ffn_gate(n, c):
                dve.wait_ge(f_g, n * NC + (c + 1))
                if c == 0:
                    dve.wait_ge(f_o, at("f_o", n))
                nc.vector.scalar_tensor_tensor(out=fh[0:CH[c], c], in0=bank((4, 6, 4)[c])[0:CH[c], :],
                                               scalar=b1s[0:CH[c], c:c + 1], in1=fg[0:CH[c], c % 2],
                                               op0=ALU.add, op1=ALU.mult).then_inc(f_h, 1)

            def ffn_add(n, b):
                dve.wait_ge(f_o, at("f_o", n + 1))
                xb = x[:, bass.ds(b * SEQ, SEQ)]
                nc.vector.tensor_tensor(xb, xb, bank(6), ALU.add).then_inc(f_x, 1)

            with dve.Fori(0, L) as l:
                fold(l + 1)
                scale_tables(l)
                layer_blocks(dve, l, turn)
                n0 = l * NB
                ffn_bias(l)
                ffn_deviation(n0)
                ffn_rstd(n0)
                ffn_norm(n0)
                if NB > 1:
                    with dve.Fori(0, NB - 1) as b:
                        n = l * NB + b
                        ffn_deviation(n + 1)
                        ffn_gate(n, 0)
                        ffn_rstd(n + 1)
                        ffn_gate(n, 1)
                        ffn_gate(n, 2)
                        ffn_norm(n + 1)
                        ffn_add(n, b)
                for c in range(NC):
                    ffn_gate(l * NB + (NB - 1), c)
                ffn_add(l * NB + (NB - 1), NB - 1)
            dve.wait_ge(f_x, at("f_x", L * NB))
            with dve.Fori(0, NB) as b:
                xb = x[:, bass.ds(b * SEQ, SEQ)]
                nc.vector.tensor_tensor(xb, xb, acc[:, bass.ds(b * SEQ, SEQ)], ALU.add).then_inc(s_fin, 1)

        @block.tensor
        def _(pe):
            def fold(n):
                pe.wait_ge(s_wa, (n + 1) * 48)
                for h in range(H):
                    rows = slice(h % 2 * DH, (h % 2 + 1) * DH)
                    to = slot(h)
                    m = nc.tensor.matmul(bank(2 + to // 4)[:, to % 4 * DIM:(to % 4 + 1) * DIM], wv[rows, h // 2], wo[rows, h // 2],
                                         start=True, stop=True)
                m.then_inc(s_m, 1)

            def project(src, i, pool):
                for s in range(2):
                    m = nc.tensor.matmul(pool[:, s * 512:(s + 1) * 512], src,
                                         wqk[:, i * INNER + s * 512:i * INNER + (s + 1) * 512], start=True, stop=True)
                return m

            def transposes(i, pool):
                for a in range(PAIRS):
                    t = nc.tensor.transpose(pool[:, a * P:(a + 1) * P], qn[:, i * INNER + a * P:i * INNER + (a + 1) * P], ident)
                return t

            pe.wait_ge(s_ld, 16 * (4 + NB))
            pe.wait_ge(s_avg, 1)
            pe.wait_ge(s_mask, 3)
            pe.wait_ge(s_row, 2)
            fold(0)
            pe.wait_ge(s_msb, 1)

            with pe.Fori(0, NB) as b:
                pe.wait_ge(a_xn, b + 1)
                for u in range(NU):
                    t = nc.tensor.transpose(ps_x[:, u * P:(u + 1) * P], xnb[:, u * P:(u + 1) * P], ident)
                t.then_inc(a_xt, 1)
                pe.wait_ge(a_xtsb, b + 1)
                for u in range(NU + 1):
                    if u < NU:
                        g = b * NU + u
                        pe.wait_ge(a_qk, at("a_qk", g * 2))
                        project(xnT[:, u * P:(u + 1) * P], 0, pool0).then_inc(a_pj, 1)
                        project(xnT[:, u * P:(u + 1) * P], 1, pool1).then_inc(a_pj, 1)
                    if u >= 1:
                        g = b * NU + (u - 1)
                        pe.wait_ge(a_qn, at("a_qn", g + 1))
                        pe.wait_ge(a_tsb, at("a_tsb", g * 2))
                        transposes(0, pool2).then_inc(a_t, 1)
                        transposes(1, pool3).then_inc(a_t, 1)
                pe.wait_ge(a_tsb, at("a_tsb", (b + 1) * (2 * NU)))

                def scores(n):
                    h, qb = n // NU, n % NU
                    rows = slice(h % 2 * DH, (h % 2 + 1) * DH)
                    if n >= 3:
                        pe.wait_ge(a_e, b * TILES + (n - 2))
                    nc.tensor.matmul(bank(sbank[n % 3]), qTA[rows, h // 2, qb * P:(qb + 1) * P], kTA[rows, h // 2, :],
                                     start=True, stop=True).then_inc(a_s, 1)

                scores(0)
                scores(1)
                for n in range(TILES + 2):
                    if n + 2 < TILES:
                        scores(n + 2)
                    if n < TILES:
                        pe.wait_ge(a_p, b * TILES + (n + 1))
                        if n >= 2:
                            pe.wait_ge(a_ptsb, b * TILES + (n - 1))
                        for k in range(NU):
                            t = nc.tensor.transpose(bank(2 + n % 2)[:, k * P:(k + 1) * P], eA[:, n % 2, k * P:(k + 1) * P], ident)
                        t.then_inc(a_pt, 1)
                    if n >= NU and n % NU == 0:
                        h = n // NU - 1
                        pe.wait_ge(a_ptsb, b * TILES + n)
                        for k in range(NU):
                            m = nc.tensor.matmul(bank(4 + h % 2), xnb[:, k * P:(k + 1) * P], pTA[:, h % 2, k, :],
                                                 start=(k == 0), stop=(k == NU - 1))
                        m.then_inc(a_y, 1)
                    if n >= NU + 1 and (n - 1) % NU == 0:
                        h = (n - 1) // NU - 1
                        pe.wait_ge(a_ysb, b * H + (h + 1))
                        for k in range(NU):
                            m = nc.tensor.matmul(ps_out[:, k * DIM:(k + 1) * DIM], yA[:, h % 2 * SEQ + k * P:h % 2 * SEQ + (k + 1) * P],
                                                 mh[:, slot(h)], start=(h == 0 and k == 0), stop=(h == H - 1), skip_group_check=True)
                        if h == H - 1:
                            m.then_inc(a_o, 1)

            def turn(g, lb, c, last):
                has = stages(c, last)
                if has[2]:
                    n = c + 2
                    u = n % NU
                    block_T = xsT[:, WIN + u * P:WIN + (u + 1) * P]
                    pe.wait_ge(l_xsT, g + (n + 1))
                    pe.wait_ge(l_sub, at("l_sub", g + (n - 1)))
                    project(block_T, 0, pool0).then_inc(l_pq, 1)
                    pe.wait_ge(l_y1sb, at("l_y1sb", g + (n - 2)))
                    project(block_T, 1, pool1).then_inc(l_pk, 1)
                if has[1]:
                    n = c + 1
                    pe.wait_ge(l_qn, at("l_qn", g + (n + 1)))
                    if has[2]:
                        pe.wait_ge(l_q, g + (n + 2))
                    else:
                        pe.wait_ge(l_sub, at("l_sub", g + n))
                    transposes(0, pool0).then_inc(l_tq, 1)
                if has[1]:
                    n = c + 1
                    if has[2]:
                        pe.wait_ge(l_k, g + (n + 2))
                    else:
                        pe.wait_ge(l_y1sb, at("l_y1sb", g + (n - 1)))
                    transposes(1, pool1).then_inc(l_tk, 1)
                if has[0]:
                    n = c
                    pe.wait_ge(l_p, at("l_p", g + (n + 1)))
                    pe.wait_ge(l_y0sb, at("l_y0sb", g + n))
                    for a in range(PAIRS):
                        t = nc.tensor.transpose(pool2[:, a * P:(a + 1) * P], pn[:, a * P:(a + 1) * P], ident)
                    t.then_inc(l_pt, 1)
                if has[2]:
                    n = c + 2
                    pe.wait_ge(l_xdup, g + (n + 1))
                    for w in range(NW):
                        t = nc.tensor.transpose(ps_x[:, w * DIM:(w + 1) * DIM], xdup[:, w].rearrange("p a k -> p (a k)"), ident)
                    t.then_inc(l_xw, 1)
                if has[1]:
                    n = c + 1
                    u = n % NU
                    pe.wait_ge(l_qT, g + (n + 1))
                    pe.wait_ge(l_kT, g + (n + 1))
                    pe.wait_ge(l_kT2, g + (n + 1))
                    for s in range(2):
                        nc.tensor.matmul(pool0[:, s * 512:(s + 1) * 512], identb[:],
                                         mask[:, 0 if u == 0 else 1].rearrange("p h k -> p (h k)"), start=True, stop=False,
                                         skip_group_check=True)
                    for a in range(PAIRS):
                        for w in range(NW):
                            key0 = u * P + w * WIN
                            m = nc.tensor.matmul(pool0[w * WIN:(w + 1) * WIN, a * 2 * KEYS:(a + 1) * 2 * KEYS],
                                                 qT[:, a, w * WIN:(w + 1) * WIN], kpad[:, 2 * a:2 * a + 2, key0:key0 + KEYS],
                                                 start=False, stop=True, skip_group_check=True)
                    m.then_inc(l_s, 1)
                if has[0]:
                    n = c
                    pe.wait_ge(l_pT, g + (n + 1))
                    pe.wait_ge(l_xwsb, at("l_xwsb", g + (n + 1)))
                    windows_times(0, n, pool2).then_inc(l_y0, 1)
                if has[3]:
                    n = c + 3
                    pe.wait_ge(l_xin, g + (n + 1))
                    pe.wait_ge(l_xwsb, at("l_xwsb", g + n))
                    nc.tensor.transpose(ps_x[:, 0:P], xin[:, n % 2], ident).then_inc(l_xt, 1)
                if has[0]:
                    n = c
                    if has[1]:
                        pe.wait_ge(l_kT, g + (n + 2))
                        pe.wait_ge(l_kT2, g + (n + 2))
                    else:
                        pe.wait_ge(l_y1sb, at("l_y1sb", g + n))
                    windows_times(1, n, pool1).then_inc(l_y1, 1)
                if has[0]:
                    n = c
                    pe.wait_ge(l_y0sb, at("l_y0sb", g + (n + 1)))
                    pe.wait_ge(l_x, at("l_x", g + n))
                    for odd in range(2):
                        if odd:
                            pe.wait_ge(l_y1sb, at("l_y1sb", g + (n + 1)))
                        for h in range(odd, H, 2):
                            m = nc.tensor.matmul(ps_out[:, 0:DIM], y[:, h], mh[:, slot(h)], start=(h == 0), stop=(h == H - 1))
                    m.then_inc(l_o, 1)

            def windows_times(odd, n, pool):
                rows = slice(odd * KEYS, (odd + 1) * KEYS)
                for w in range(NW):
                    m = nc.tensor.matmul(pool[:, w * PAIRS * WIN:(w + 1) * PAIRS * WIN], xw[rows, n % NU, w],
                                         pT[rows, :, w * WIN:(w + 1) * WIN], start=True, stop=True)
                return m

            def ffn_mean(n):
                pe.wait_ge(f_in, n + 1)
                for k in range(NU):
                    t = nc.tensor.transpose(bank(0)[:, k * P:(k + 1) * P], fin[:, k * P:(k + 1) * P], ident)
                t.then_inc(f_xt, 1)
                pe.wait_ge(f_T, n + 1)
                nc.tensor.matmul(bank(1), onesd[:], fT, start=True, stop=True).then_inc(f_mu, 1)

            def ffn_variance(n):
                pe.wait_ge(f_sq, n + 1)
                for k in range(NU):
                    m = nc.tensor.matmul(bank(2)[:, k:k + 1], fsq[:, k * P:(k + 1) * P], onesd[:, 0:1], start=True, stop=True)
                m.then_inc(f_var, 1)

            def ffn_spread(n):
                pe.wait_ge(f_dg, n + 1)
                nc.tensor.matmul(bank(3), onesd[:], fdg, start=True, stop=True).then_inc(f_bc, 1)

            def ffn_up(n, c):
                if c == 0:
                    pe.wait_ge(f_xn, at("f_xn", n + 1))
                elif c == 1:
                    pe.wait_ge(f_x, at("f_x", n))
                else:
                    pe.wait_ge(f_h, at("f_h", n * NC + 1))
                for half in range(2):
                    m = nc.tensor.matmul(bank((4, 6, 4)[c] + half)[0:CH[c], :],
                                         w1s[:, half * FH + c * P:half * FH + c * P + CH[c]], fxn, start=True, stop=True)
                m.then_inc(f_u, 1)

            def ffn_down(n):
                pe.wait_ge(f_h, at("f_h", n * NC + NC))
                for k in range(NU):
                    for c in range(NC):
                        rows = P if c < NC - 1 else ONES_ROW + 1
                        m = nc.tensor.matmul(bank(6)[:, k * DIM:(k + 1) * DIM], fh[0:rows, c, k * P:(k + 1) * P],
                                             w2[0:rows, c], start=(c == 0), stop=(c == NC - 1))
                m.then_inc(f_o, 1)

            with pe.Fori(0, L) as l:
                fold(l + 1)
                pe.wait_ge(s_msb, l + 2)
                layer_blocks(pe, l, turn)
                pe.wait_ge(l_x, at("l_x", (l + 1) * NBLK))
                pe.wait_ge(s_wf, (l + 1) * 48)
                pe.wait_ge(f_w, l + 1)
                for half in range(2):
                    for c in range(NC):
                        col = half * NC + c
                        m = nc.tensor.matmul(bank(1)[0:CH[c], col:col + 1],
                                             w1[:, half * FH + c * P:half * FH + c * P + CH[c]], sm[:, 1:2], start=True, stop=True)
                m.then_inc(f_b, 1)
                pe.wait_ge(f_bs, l + 1)
                ffn_mean(l * NB)
                ffn_variance(l * NB)
                ffn_spread(l * NB)
                if NB > 1:
                    with pe.Fori(0, NB - 1) as b:
                        n = l * NB + b
                        ffn_mean(n + 1)
                        ffn_up(n, 0)
                        ffn_variance(n + 1)
                        ffn_up(n, 1)
                        ffn_up(n, 2)
                        ffn_spread(n + 1)
                        ffn_down(n)
                n = l * NB + (NB - 1)
                for c in range(NC):
                    ffn_up(n, c)
                ffn_down(n)


def constants():
    q = np.arange(P)[:, None]
    key = np.arange(KEYS)[None, :]
    inside = (q % WIN <= key) & (key <= q % WIN + WIN)
    first = inside & ((q >= WIN) | (key >= WIN))
    masks = [np.where(m, 0.0, NEG) for m in (first, inside)]
    half = np.arange(0, DH, 2, dtype=np.float32)
    inv_freq = (np.float32(1.0) / np.float32(10000.0) ** (half / np.float32(DH))).astype(np.float32)
    t = np.arange(SEQ, dtype=np.float32)
    freqs = t[:, None] * inv_freq[None, :]
    freqs = np.concatenate([freqs, freqs], -1)
    base = (half + np.float32(0.4 * DH)) / np.float32(1.4 * DH)
    scale = base[None, :] ** ((t - SEQ // 2) / np.float32(WIN // 2))[:, None]
    scale = np.concatenate([scale, scale], -1)
    sign = np.where(np.arange(DH) < DH // 2, -1.0, 1.0)
    cos, sin = np.cos(freqs), np.sin(freqs) * sign
    tables = np.stack([np.stack([cos * scale, cos / scale], 1), np.stack([sin * scale, sin / scale], 1)])
    tables = tables.reshape(2, NU, P, 2, DH).transpose(2, 0, 1, 3, 4).reshape(P, -1)
    return np.ascontiguousarray(np.concatenate([np.eye(P)] + masks + [tables], 1).astype(np.float32))


def pairs_of_heads(w):
    lead = w.shape[:-2]
    n = w.shape[-1]
    w = w.reshape(*lead, PAIRS, P, n)
    return np.ascontiguousarray(np.moveaxis(w, -3, -2)).reshape(*lead, P, PAIRS * n)


def kernel(**inputs):
    import concourse.bacc as bacc
    from concourse.bass_utils import run_bass_kernel_spmd

    get = {k: np.asarray(v) for k, v in inputs.items()}
    x_in = get["L0_attn_x"]
    wqkv_a, wqkv = get["L0_attn_w_qkv"], get["L0_ffn_Wqkv"]
    L = wqkv.shape[0]
    w2 = get["L0_ffn_W2"]
    w2p = np.zeros((L, NC * P, DIM), np.float32)
    w2p[:, 0:FH] = w2
    w2p[:, (NC - 1) * P + ONES_ROW] = get["L0_ffn_b2"]
    small = np.zeros((L, P, 2 + 2 * NC), np.float32)
    small[:, :, 0] = get["L0_ffn_ln_g"]
    small[:, :, 1] = get["L0_ffn_ln_b"]
    for half in range(2):
        for c in range(NC):
            lo = half * FH + c * P
            small[:, 0:CH[c], 2 + half * NC + c] = get["L0_ffn_b1"][:, lo:lo + CH[c]]
    arrays = {
        "x_in": x_in,
        "consts": constants(),
        "a_logit": get["L0_attn_logit_scale"].reshape(H),
        "a_bout": get["L0_attn_b_out"],
        "a_wqk": wqkv_a[:, 0:2 * INNER],
        "a_wv": pairs_of_heads(wqkv_a[:, 2 * INNER:].T),
        "a_wo": pairs_of_heads(get["L0_attn_w_out"]),
        "l_wqk": wqkv[:, :, 0:2 * INNER],
        "l_wv": pairs_of_heads(wqkv[:, :, 2 * INNER:].transpose(0, 2, 1)),
        "l_wo": pairs_of_heads(get["L0_ffn_Wo"]),
        "l_scale": np.concatenate([get["L0_ffn_q_scale"], get["L0_ffn_k_scale"]], 1),
        "l_w1": get["L0_ffn_W1"],
        "l_w2": w2p.reshape(L, NC, P, DIM).transpose(0, 2, 1, 3).reshape(L, P, NC * DIM),
        "l_small": small,
    }
    arrays = {k: np.ascontiguousarray(v) for k, v in arrays.items()}
    nc = bacc.Bacc("TRN2", target_bir_lowering=False, num_devices=1)
    aps = {k: nc.dram_tensor(f"in_{k}", v.shape, F32, kind="ExternalInput").ap() for k, v in arrays.items()}
    out = nc.dram_tensor("out_0_dram", x_in.shape, F32, kind="ExternalOutput").ap()
    build(nc, out=out, **aps)
    r = run_bass_kernel_spmd(nc, [{f"in_{k}": v for k, v in arrays.items()}], core_ids=[0])
    return r.results[0]["out_0_dram"]
```

```python
from contextlib import ExitStack

import numpy as np
import concourse.bass as bass
from concourse import mybir

P = 128
ALU = mybir.AluOpType
ACT = mybir.ActivationFunctionType
F32 = mybir.dt.float32
I32 = mybir.dt.int32
BF16 = mybir.dt.bfloat16
X = mybir.AxisListType.X

DIM = 128
H, DH = 16, 64
PAIRS = H // 2
INNER = H * DH
WIN = 32
KEYS = 2 * WIN
SEQ = 512
NU = SEQ // P
NW = P // WIN
QK_SCALE = 8.0
MAX_LOG_SCALE = float(np.log(1.0 / 0.01))
NORM_FLOOR = 1e-24
EPS = 1e-5
FH = int(DIM * 4 * 2 / 3)
CH = [P, P, FH - 2 * P]
NC = len(CH)
ONES_ROW = 96
NEG = -1e30
RS = 11
RS_POOL = 12
TILES = H * NU


def build(nc, x_in, consts, a_logit, a_bout, a_wqk, a_wv, a_wo, l_wqk, l_wv, l_wo, l_scale, l_w1, l_w2, l_small, out):
    NB = x_in.shape[0]
    L = l_w1.shape[0]
    NBLK = NB * NU

    x_dram = x_in.rearrange("b (k p) d -> p (b k) d", p=P)
    out_dram = out.rearrange("b (k p) d -> b p k d", p=P)

    with ExitStack() as ctx:
        def sb(name, shape, dt=F32):
            return ctx.enter_context(nc.sbuf_tensor(name, shape, dt))

        credits = {}

        def sem(name, credit=0):
            s = ctx.enter_context(nc.semaphore(name))
            credits[name] = (s, credit)
            return s

        def at(name, n):
            return n + credits[name][1]

        x = sb("x", [P, NBLK * DIM])
        acc = sb("acc", [P, NBLK * DIM])
        xin = sb("xin", [P, 2, DIM])
        xsT = sb("xsT", [P, WIN + SEQ + 1])
        xdup = sb("xdup", [P, NW, 2, KEYS])
        xw = sb("xw", [P, NU, NW, DIM])
        qk = sb("qk", [P, 2 * INNER])
        sq = sb("sq", [P, 2 * INNER])
        t12 = sb("t12", [P, 4 * INNER])
        qn = sb("qn", [P, 2 * INNER])
        qT = sb("qT", [P, PAIRS, P])
        kpad = sb("kpad", [P, H, WIN + SEQ])
        es = sb("es", [P, INNER])
        pn = sb("pn", [P, INNER])
        pT = sb("pT", [P, PAIRS, P])
        y = sb("y", [P, H, P])
        wqk = sb("wqk", [P, 2 * INNER])
        wv = sb("wv", [P, PAIRS, DIM])
        wo = sb("wo", [P, PAIRS, DIM])
        mh = sb("mh", [P, H, DIM])
        cst = sb("cst", [P, P + 2 * KEYS])
        tab = sb("tab", [P, 2, NU, 2, DH])
        tabl = sb("tabl", [P, 2, NU, 2, DH])
        qks = sb("qks", [P, 2, DH])
        mask = sb("mask", [P, 2, H // 2, KEYS], BF16)
        identb = sb("identb", [P, P], BF16)
        onesd = sb("onesd", [P, P])
        ss = sb("ss", [P, 2 * H])
        c15 = sb("c15", [P, 2 * H])
        rn = sb("rn", [P, 2 * H])
        rt = sb("rt", [P, 2 * H])
        mx = sb("mx", [P, H])
        den = sb("den", [P, H])
        rden = sb("rden", [P, H])
        sc = sb("sc", [P, H])
        boutb = sb("boutb", [P, DIM])
        st = sb("st", [P, NU, 6])
        agg = sb("agg", [P, NU, 2])
        mv = sb("mv", [P, NBLK, 2])
        av = sb("av", [P, NBLK])
        rstd = sb("rstd", [P, NBLK])
        artmp = sb("artmp", [P, NBLK])
        ass = sb("ass", [P, 2, 2 * H])
        arn = sb("arn", [P, 2, 2 * H])
        art = sb("art", [P, 2, 2 * H])
        amx = sb("amx", [P, 4])
        anm = sb("anm", [P, 4])
        aden = sb("aden", [P, 4])
        ardn = sb("ardn", [P, 4])
        w1 = sb("w1", [P, 2 * FH])
        w1s = sb("w1s", [P, 2 * FH])
        w2 = sb("w2", [P, NC, DIM])
        sm = sb("sm", [P, 2 + 2 * NC])
        b1s = sb("b1s", [P, 2 * NC])
        fh = sb("fh", [P, 2, NC, SEQ])

        ident = cst[:, 0:P]
        t1 = t12[:, 0:2 * INNER]
        t2 = t12[:, 2 * INNER:4 * INNER]
        kflat = kpad[:].rearrange("p h c -> p (h c)")
        qTA = kflat[:, 0:PAIRS * SEQ].rearrange("p (h c) -> p h c", h=PAIRS)
        kTA = kflat[:, PAIRS * SEQ:2 * PAIRS * SEQ].rearrange("p (h c) -> p h c", h=PAIRS)
        pTA = t12[:].rearrange("p (s k q) -> p s k q", s=2, k=NU)
        eA = es[:].rearrange("p (s k) -> p s k", s=2)
        yA = y[:].rearrange("p h c -> p (h c)")
        xnb = pn[:, 0:SEQ]
        qkA, sqA = (qk[:], t1), (sq[:], t2)
        qnA = (qn[:], xw[:].rearrange("p u w d -> p (u w d)"))
        xnT = xsT[:, WIN:WIN + SEQ]
        fin = qk[:, 0:SEQ]
        fT = qk[:, SEQ:2 * SEQ]
        fdg = qk[:, 2 * SEQ:3 * SEQ]
        fd = sq[:, 0:SEQ]
        fsq = sq[:, SEQ:2 * SEQ]
        fxn = sq[:, 2 * SEQ:3 * SEQ]
        fg = t12[:, 0:2 * SEQ].rearrange("p (s c) -> p s c", s=2)

        ps = ctx.enter_context(nc.psum_tensor("ps", [P, 8 * 512], F32))

        def bank(n, w=1):
            return ps[:, 512 * n:512 * (n + w)]

        pool0, pool1, pool2, pool3 = bank(0, 2), bank(2, 2), bank(4, 2), bank(6, 2)
        ps_out, ps_x = bank(6), bank(7)
        sbank = (0, 1, 7)

        s_ld = sem("s_ld")
        s_wa = sem("s_wa")
        s_wf = sem("s_wf")
        s_wqs = sem("s_wqs")
        s_avg = sem("s_avg")
        s_mask = sem("s_mask")
        s_row = sem("s_row")
        s_zero = sem("s_zero")
        s_sc = sem("s_sc")
        s_m = sem("s_m")
        s_msb = sem("s_msb")
        s_tab = sem("s_tab")
        s_rs = sem("s_rs")
        l_fl = sem("l_fl")
        l_gs = sem("l_gs")
        l_rs = sem("l_rs")
        a_st = sem("a_st")
        a_mv = sem("a_mv")
        a_mvc = sem("a_mvc", 1)
        a_xn = sem("a_xn")
        a_xcp = sem("a_xcp", 1)
        a_xt = sem("a_xt")
        a_xtsb = sem("a_xtsb")
        a_pj = sem("a_pj")
        a_qk = sem("a_qk", 1)
        a_sq = sem("a_sq")
        a_ss = sem("a_ss")
        a_fl = sem("a_fl")
        a_gs = sem("a_gs")
        a_rs = sem("a_rs")
        a_dev = sem("a_dev")
        a_qn = sem("a_qn", 2)
        a_t = sem("a_t", 3)
        a_tsb = sem("a_tsb", 1)
        a_s = sem("a_s")
        a_mx = sem("a_mx")
        a_nm = sem("a_nm")
        a_e = sem("a_e")
        a_rd = sem("a_rd")
        a_p = sem("a_p")
        a_pt = sem("a_pt")
        a_ptsb = sem("a_ptsb")
        a_y = sem("a_y")
        a_ysb = sem("a_ysb")
        a_o = sem("a_o")
        a_b = sem("a_b")
        a_acc = sem("a_acc", 1)
        l_xin = sem("l_xin")
        l_xt = sem("l_xt", 2)
        l_xsT = sem("l_xsT")
        l_xdup = sem("l_xdup")
        l_xw = sem("l_xw")
        l_xwsb = sem("l_xwsb", 1)
        l_pq = sem("l_pq")
        l_pk = sem("l_pk")
        l_q = sem("l_q")
        l_k = sem("l_k")
        l_sq = sem("l_sq", 1)
        l_ss = sem("l_ss", 1)
        l_rp = sem("l_rp", 2)
        l_rot = sem("l_rot")
        l_qn = sem("l_qn", 1)
        l_tq = sem("l_tq")
        l_tk = sem("l_tk", 1)
        l_qT = sem("l_qT")
        l_kT = sem("l_kT")
        l_kT2 = sem("l_kT2")
        l_s = sem("l_s", 1)
        l_mx = sem("l_mx")
        l_sub = sem("l_sub", 2)
        l_e = sem("l_e")
        l_den = sem("l_den")
        l_rd = sem("l_rd")
        l_p = sem("l_p", 1)
        l_pt = sem("l_pt", 1)
        l_pT = sem("l_pT")
        l_y0 = sem("l_y0")
        l_y1 = sem("l_y1")
        l_y0sb = sem("l_y0sb", 1)
        l_y1sb = sem("l_y1sb", 3)
        l_o = sem("l_o", 1)
        l_x = sem("l_x", 1)
        f_w = sem("f_w")
        f_b = sem("f_b")
        f_bs = sem("f_bs")
        f_in = sem("f_in")
        f_xt = sem("f_xt", 1)
        f_T = sem("f_T")
        f_mu = sem("f_mu")
        f_d = sem("f_d")
        f_sq = sem("f_sq")
        f_var = sem("f_var")
        f_dg = sem("f_dg")
        f_bc = sem("f_bc")
        f_xn = sem("f_xn", 1)
        f_u = sem("f_u", 1)
        f_g = sem("f_g")
        f_h = sem("f_h", 2)
        f_o = sem("f_o", 2)
        f_x = sem("f_x", 2)
        s_fin = sem("s_fin")
        s_out = sem("s_out")

        def keys(odd, u):
            rows = slice(odd * DH, (odd + 1) * DH)
            return (kpad[rows].rearrange("p (a s) c -> p a s c", s=2)[:, :, odd, WIN + u * P:WIN + (u + 1) * P],
                    pool1[rows].rearrange("p (h c) -> p h c", h=PAIRS))

        def layer_blocks(eng, l, turn):
            g0 = l * NBLK
            for c in (-3, -2, -1):
                turn(g0, 0, c, False)
            if NB > 1:
                with eng.Fori(0, NB - 1) as b:
                    for c in range(NU):
                        turn(g0 + b * NU, b * NU, c, False)
            for c in range(NU):
                turn(g0 + (NB - 1) * NU, (NB - 1) * NU, c, True)

        def stages(c, last):
            return [c + k >= 0 and (not last or c + k < NU) for k in range(4)]

        def slot(h):
            return h % 2 * PAIRS + h // 2

        def heads(ap, n):
            return ap.rearrange("p (h d) -> p h d", h=n)

        def newton(pool, done, count, root, half, tmp):
            for step in range(RS_POOL):
                to, a, b, op = ((tmp, root, root, ALU.mult), (tmp, tmp, half, ALU.mult),
                                (tmp, c15[:], tmp, ALU.subtract), (root, root, tmp, ALU.mult))[step % 4]
                if step:
                    pool.wait_ge(done, count * RS_POOL + step)
                nc.gpsimd.tensor_tensor(to, a, b, op).then_inc(done, 1)

        def rsqrt(src, dst, tmp, calls, pre, const):
            steps = [0]

            def link(ins):
                steps[0] += 1
                ins.then_inc(s_rs, 1)
                if steps[0] < RS:
                    nc.vector.wait_ge(s_rs, calls * RS + steps[0])

            link(nc.vector.tensor_scalar(src[1], src[0], const, None, pre))
            v = src[1]
            link(nc.vector.tensor_scalar(dst.bitcast(I32), v.bitcast(I32), -0.5, float(0x5F3759DF), ALU.mult, ALU.add))
            for _ in range(3):
                link(nc.vector.scalar_tensor_tensor(out=tmp, in0=dst, scalar=-0.5, in1=dst, op0=ALU.mult, op1=ALU.mult))
                link(nc.vector.tensor_tensor(tmp, tmp, v, ALU.mult))
                link(nc.vector.scalar_tensor_tensor(out=dst, in0=tmp, scalar=1.5, in1=dst, op0=ALU.add, op1=ALU.mult))

        block = ctx.enter_context(nc.Block())

        @block.sync
        def _(sp):
            for s, credit in credits.values():
                if credit:
                    sp.sem_inc(s, credit)
            sp.dma_start(cst[:], consts[:, 0:P + 2 * KEYS]).then_inc(s_ld, 16)
            sp.dma_start(sc[:], a_logit.partition_broadcast(P)).then_inc(s_ld, 16)
            sp.dma_start(boutb[:], a_bout.partition_broadcast(P)).then_inc(s_ld, 16)
            sp.dma_start(tab[:].rearrange("p a b c d -> p (a b c d)"), consts[:, P + 2 * KEYS:]).then_inc(s_ld, 16)
            for b in range(NB):
                sp.dma_start(acc[:, b * SEQ:(b + 1) * SEQ].rearrange("p (k d) -> p k d", k=NU),
                             x_dram[:, b * NU:(b + 1) * NU, :]).then_inc(s_ld, 16)

            def attention_weights(wqk_dram, wv_dram, wo_dram):
                sp.dma_start(wqk[:], wqk_dram).then_inc(s_wa, 16)
                sp.dma_start(wv[:].rearrange("p h d -> p (h d)"), wv_dram).then_inc(s_wa, 16)
                sp.dma_start(wo[:].rearrange("p h d -> p (h d)"), wo_dram).then_inc(s_wa, 16)

            def layer_row(ap, l):
                return ap[bass.ds(l, 1)].rearrange("a p n -> (a p) n")

            def layer_attention_weights(l):
                attention_weights(layer_row(l_wqk, l), layer_row(l_wv, l), layer_row(l_wo, l))

            def ffn_weights(l):
                sp.dma_start(w1[:], layer_row(l_w1, l)).then_inc(s_wf, 16)
                sp.dma_start(w2[:].rearrange("p c d -> p (c d)"), layer_row(l_w2, l)).then_inc(s_wf, 16)
                sp.dma_start(sm[:], layer_row(l_small, l)).then_inc(s_wf, 16)
                sp.dma_start(qks[:].rearrange("p a d -> p (a d)"),
                             l_scale[bass.ds(l, 1)].rearrange("a n -> (a n)").partition_broadcast(P)).then_inc(s_wqs, 16)

            attention_weights(a_wqk, a_wv, a_wo)
            ffn_weights(0)
            sp.wait_ge(a_pj, 2 * NBLK)
            sp.wait_ge(s_m, 1)
            layer_attention_weights(0)
            if L > 1:
                with sp.Fori(1, L) as l:
                    sp.wait_ge(l_pk, l * NBLK)
                    layer_attention_weights(l)
                    sp.wait_ge(f_x, at("f_x", l * NB))
                    ffn_weights(l)
            with sp.Fori(0, NB) as b:
                sp.wait_ge(s_fin, b + 1)
                sp.dma_start(out_dram[bass.ds(b, 1)].rearrange("b p k d -> p (b k) d"),
                             x[:, bass.ds(b * SEQ, SEQ)].rearrange("p (k d) -> p k d", k=NU)).then_inc(s_out, 16)
            sp.wait_ge(s_out, 16 * NB)

        @block.gpsimd
        def _(pool):
            nc.gpsimd.memset(onesd[:], 1.0 / DIM).then_inc(s_avg, 1)
            nc.gpsimd.memset(c15[:], 1.5).then_inc(s_avg, 1)
            pool.wait_ge(s_avg, 2)
            with pool.Fori(0, NB) as b:
                pool.wait_ge(a_xn, b + 1)
                nc.gpsimd.tensor_copy(x[:, bass.ds(b * SEQ, SEQ)], xnb).then_inc(a_xcp, 1)
                for u in range(NU):
                    g = b * NU + u
                    pool.wait_ge(a_gs, g + 1)
                    newton(pool, a_rs, g, arn[:, u % 2], ass[:, u % 2], art[:, u % 2])
            pool.wait_ge(a_acc, at("a_acc", NB))
            nc.gpsimd.memset(xsT[:], 0.0).then_inc(s_zero, 1)
            nc.gpsimd.memset(kpad[:], 0.0).then_inc(s_zero, 1)

            def turn(g, lb, c, last):
                has = stages(c, last)
                if has[2]:
                    n = c + 2
                    for i in range(2):
                        half = slice(i * INNER, (i + 1) * INNER)
                        pool.wait_ge(l_rp, at("l_rp", (g + n) * 2 + (i + 1)))
                        rotated = nc.gpsimd.tensor_tensor(t1[:, half], t1[:, half], t2[:, half], ALU.add)
                    rotated.then_inc(l_rot, 1)
                    pool.wait_ge(l_rot, g + (n + 1))
                    pool.wait_ge(l_gs, g + (n + 1))
                    newton(pool, l_rs, g + n, rn[:], ss[:], rt[:])
                if has[1]:
                    n = c + 1
                    pool.wait_ge(l_rd, g + (n + 1))
                    pool.wait_ge(l_pt, at("l_pt", g + n))
                    nc.gpsimd.tensor_tensor(heads(pn[:], H), heads(es[:], H),
                                            rden[:].unsqueeze(2).to_broadcast([P, H, KEYS]), ALU.mult).then_inc(l_p, 1)

            with pool.Fori(0, L) as l:
                layer_blocks(pool, l, turn)

        @block.scalar
        def _(act):
            act.wait_ge(s_ld, 16 * (4 + NB))
            act.activation(identb[:], ident, ACT.Copy).then_inc(s_mask, 1)
            for m in range(2):
                act.activation(mask[:, m], cst[:, P + m * KEYS:P + (m + 1) * KEYS].unsqueeze(1)
                               .to_broadcast([P, H // 2, KEYS]), ACT.Copy).then_inc(s_mask, 1)
            act.wait_ge(s_sc, 1)
            act.activation(sc[:], sc[:], ACT.Exp).then_inc(s_sc, 1)
            act.wait_ge(s_sc, 2)

            with act.Fori(0, NB) as b:
                act.wait_ge(a_xt, b + 1)
                act.activation(xnT, ps_x, ACT.Copy).then_inc(a_xtsb, 1)
                for u in range(NU + 2):
                    if u < NU:
                        g = b * NU + u
                        act.wait_ge(a_qn, at("a_qn", g - 1))
                        for i in range(2):
                            act.wait_ge(a_pj, g * 2 + (i + 1))
                            act.activation(qkA[u % 2][:, i * INNER:(i + 1) * INNER], (pool0, pool1)[i], ACT.Copy).then_inc(a_qk, 1)
                        act.wait_ge(a_qk, at("a_qk", g * 2 + 2))
                        act.activation(sqA[u % 2], qkA[u % 2], ACT.Square).then_inc(a_sq, 1)
                    if u >= 2:
                        g = b * NU + (u - 2)
                        for i in range(2):
                            act.wait_ge(a_t, at("a_t", g * 2 + (i + 1)))
                            act.activation((qTA, kTA)[i][:, :, (u - 2) * P:(u - 1) * P],
                                           (pool2, pool3)[i].rearrange("p (h c) -> p h c", h=PAIRS),
                                           ACT.Copy).then_inc(a_tsb, 1)
                for n in range(TILES + 2 * NU):
                    if n < TILES:
                        h = n // NU
                        act.wait_ge(a_nm, b * TILES + (n + 1))
                        if n >= 2:
                            act.wait_ge(a_pt, b * TILES + (n - 1))
                        act.activation(eA[:, n % 2], bank(sbank[n % 3]), ACT.Exp, bias=anm[:, n % 4:n % 4 + 1],
                                       scale=sc[:, h:h + 1], accum_out=aden[:, n % 4:n % 4 + 1]).then_inc(a_e, 1)
                    if 1 <= n <= TILES:
                        m = n - 1
                        h, qb = m // NU, m % NU
                        act.wait_ge(a_pt, b * TILES + (m + 1))
                        if h >= 2 and qb == 0:
                            act.wait_ge(a_y, b * H + (h - 1))
                        act.activation(pTA[:, h % 2, :, qb * P:(qb + 1) * P],
                                       bank(2 + m % 2).rearrange("p (k q) -> p k q", k=NU), ACT.Copy).then_inc(a_ptsb, 1)
                    if n >= 2 * NU and n % NU == 0:
                        h = n // NU - 2
                        act.wait_ge(a_y, b * H + (h + 1))
                        act.activation(yA[:, (h % 2) * SEQ:(h % 2 + 1) * SEQ], bank(4 + h % 2), ACT.Copy).then_inc(a_ysb, 1)

            def windows(u):
                a = xsT[:, u * P:u * P + KEYS]
                return bass.AP(a.tensor, a.offset, [list(a.ap[0]), [WIN, NW], [1, KEYS]])

            def copy_y(count, odd, done_y, copied, src):
                act.wait_ge(done_y, count)
                act.activation(y[:].rearrange("p (a s) (w q) -> p s w a q", s=2, w=NW)[:, odd],
                               src.rearrange("p (w a q) -> p w a q", w=NW, a=PAIRS), ACT.Copy).then_inc(copied, 1)

            def turn(g, lb, c, last):
                has = stages(c, last)
                if has[3]:
                    n = c + 3
                    act.wait_ge(l_xt, at("l_xt", g + (n - 1)))
                    act.activation(xin[:, n % 2], x[:, bass.ds((lb + n) * DIM, DIM)], ACT.Copy).then_inc(l_xin, 1)
                if has[2]:
                    n = c + 2
                    act.wait_ge(l_rp, at("l_rp", (g + n) * 2))
                    act.wait_ge(l_sq, at("l_sq", g + n))
                    act.wait_ge(l_pq, g + (n + 1))
                    act.activation(qk[:, 0:INNER], pool0, ACT.Copy).then_inc(l_q, 1)
                if has[2]:
                    n = c + 2
                    act.wait_ge(l_q, g + (n + 1))
                    act.wait_ge(l_ss, at("l_ss", g + n))
                    act.activation(sq[:, 0:INNER], qk[:, 0:INNER], ACT.Square)
                if has[2]:
                    n = c + 2
                    act.wait_ge(l_pk, g + (n + 1))
                    act.activation(qk[:, INNER:2 * INNER], pool1, ACT.Copy).then_inc(l_k, 1)
                if has[1]:
                    n = c + 1
                    act.wait_ge(l_tq, g + (n + 1))
                    act.activation(qT[:].rearrange("p h c -> p (h c)"), pool0, ACT.Copy).then_inc(l_qT, 1)
                if has[1]:
                    n = c + 1
                    u = n % NU
                    act.wait_ge(l_tk, at("l_tk", g + (n + 1)))
                    act.activation(*keys(0, u), ACT.Copy).then_inc(l_kT, 1)
                if has[0]:
                    n = c
                    act.wait_ge(l_pt, at("l_pt", g + (n + 1)))
                    act.activation(pT[:].rearrange("p h c -> p (h c)"), pool2, ACT.Copy).then_inc(l_pT, 1)
                if has[2]:
                    n = c + 2
                    act.wait_ge(l_xw, g + (n + 1))
                    act.activation(xw[:, n % NU].rearrange("p w d -> p (w d)"), ps_x, ACT.Copy).then_inc(l_xwsb, 1)
                if has[2]:
                    n = c + 2
                    act.wait_ge(l_k, g + (n + 1))
                    act.activation(sq[:, INNER:2 * INNER], qk[:, INNER:2 * INNER], ACT.Square).then_inc(l_sq, 1)
                if has[0]:
                    copy_y(g + (c + 1), 0, l_y0, l_y0sb, pool2)
                if has[3]:
                    n = c + 3
                    u = n % NU
                    act.wait_ge(l_xt, at("l_xt", g + (n + 1)))
                    act.activation(xsT[0:DH, WIN + u * P:WIN + (u + 1) * P], ps_x[0:DH, 0:P], ACT.Copy)
                    act.activation(xsT[DH:P, WIN + 1 + u * P:WIN + 1 + (u + 1) * P], ps_x[DH:P, 0:P],
                                   ACT.Copy).then_inc(l_xsT, 1)
                    act.wait_ge(l_xsT, g + (n + 1))
                    for twice in range(2):
                        dup = act.activation(xdup[:, :, twice, :], windows(u), ACT.Copy)
                    dup.then_inc(l_xdup, 1)
                if has[0]:
                    copy_y(g + (c + 1), 1, l_y1, l_y1sb, pool1)
                if has[1]:
                    n = c + 1
                    act.wait_ge(l_sub, at("l_sub", g + (n + 1)))
                    act.activation(es[:], es[:], ACT.Exp, scale=QK_SCALE).then_inc(l_e, 1)

            def ffn_in(n, b):
                act.wait_ge(f_xt, at("f_xt", n))
                act.activation(fin, x[:, bass.ds(b * SEQ, SEQ)], ACT.Copy).then_inc(f_in, 1)

            def ffn_copy(n):
                act.wait_ge(f_xt, at("f_xt", n + 1))
                act.activation(fT[0:DH, :], bank(0)[0:DH, :], ACT.Copy)
                act.activation(fT[DH:P, 1:SEQ], bank(0)[DH:P, 0:SEQ - 1], ACT.Copy).then_inc(f_T, 1)

            def ffn_square(n):
                act.wait_ge(f_d, n + 1)
                act.activation(fsq, fd, ACT.Square).then_inc(f_sq, 1)

            def ffn_gelu(n, c):
                act.wait_ge(f_u, at("f_u", n * NC + (c + 1)))
                act.wait_ge(f_h, at("f_h", n * NC + (c - 1)))
                act.activation(fg[0:CH[c], c % 2], bank((5, 7, 5)[c])[0:CH[c], :], ACT.Gelu,
                               bias=b1s[0:CH[c], NC + c:NC + c + 1]).then_inc(f_g, 1)

            act.wait_ge(s_zero, 2)
            act.wait_ge(a_xcp, at("a_xcp", NB))
            with act.Fori(0, L) as l:
                act.wait_ge(f_x, at("f_x", l * NB))
                layer_blocks(act, l, turn)
                act.wait_ge(l_x, at("l_x", (l + 1) * NBLK))
                ffn_in(l * NB, 0)
                act.wait_ge(f_xt, at("f_xt", l * NB + 1))
                act.activation(fT[DH:P, 0:1], xsT[DH:P, 0:1], ACT.Copy)
                ffn_copy(l * NB)
                ffn_in(l * NB + 1, 1)
                ffn_square(l * NB)
                ffn_copy(l * NB + 1)
                ffn_in(l * NB + 2, 2)
                act.wait_ge(f_bs, l + 1)

                def ffn_turn(n, b, ahead):
                    ffn_gelu(n, 0)
                    if ahead >= 1:
                        ffn_square(n + 1)
                    ffn_gelu(n, 1)
                    ffn_gelu(n, 2)
                    if ahead >= 2:
                        ffn_copy(n + 2)
                    if ahead >= 3:
                        ffn_in(n + 3, b + 3)

                with act.Fori(0, NB - 3) as b:
                    ffn_turn(l * NB + b, b, 3)
                for ahead in (2, 1, 0):
                    ffn_turn(l * NB + (NB - 1 - ahead), NB - 1 - ahead, ahead)

        @block.vector
        def _(dve):
            def fold(n):
                dve.wait_ge(s_m, n + 1)
                nc.vector.tensor_copy(mh[:].rearrange("p h d -> p (h d)"), bank(2, 4)).then_inc(s_msb, 1)

            dve.wait_ge(s_ld, 16 * (4 + NB))
            nc.vector.tensor_scalar(sc[:], sc[:], MAX_LOG_SCALE, None, ALU.min).then_inc(s_sc, 1)
            nc.vector.memset(fh[DH:P, :, NC - 1], 0.0).then_inc(s_row, 1)
            dve.wait_ge(s_row, 1)
            nc.vector.memset(fh[ONES_ROW:ONES_ROW + 1, :, NC - 1], 1.0).then_inc(s_row, 1)
            fold(0)
            dve.wait_ge(s_sc, 2)

            with dve.Fori(0, NB) as b:
                for u in range(NU):
                    if u == 0:
                        dve.wait_ge(a_mvc, at("a_mvc", b))
                    stat = nc.vector.bn_stats(st[:, u], acc[:, bass.ds(b * SEQ + u * P, P)])
                stat.then_inc(a_st, 1)
                dve.wait_ge(a_st, b + 1)
                nc.vector.memset(rt[:, 0:NU], 0.0)
                for u in range(NU):
                    stat = nc.vector.bn_aggr(agg[:, u], st[:, u])
                stat.then_inc(a_mv, 1)
                dve.wait_ge(a_mv, at("a_mv", b + 1))
                nc.vector.tensor_copy(mv[:, bass.ds(b * NU, NU)], agg[:]).then_inc(a_mvc, 1)
            dve.wait_ge(a_mvc, at("a_mvc", NB))
            rsqrt((mv[:, :, 1], av[:]), rstd[:], artmp[:], 0, ALU.add, EPS)
            dve.wait_ge(s_rs, RS)
            with dve.Fori(0, NB) as b:
                tokens = acc[:, bass.ds(b * SEQ, SEQ)]
                dve.wait_ge(a_xcp, at("a_xcp", b))
                nc.vector.tensor_tensor(heads(xnb, NU), heads(tokens, NU),
                                        mv[:, bass.ds(b * NU, NU), 0:1].to_broadcast([P, NU, DIM]), ALU.subtract).then_inc(a_dev, 1)
                dve.wait_ge(a_dev, b + 1)
                nc.vector.tensor_tensor(heads(xnb, NU), heads(xnb, NU),
                                        rstd[:, bass.ds(b * NU, NU)].unsqueeze(2).to_broadcast([P, NU, DIM]),
                                        ALU.mult).then_inc(a_xn, 1)

                def norms(u):
                    g = b * NU + u
                    half = ass[:, u % 2]
                    dve.wait_ge(a_sq, g + 1)
                    nc.vector.tensor_reduce(half, heads(sqA[u % 2], 2 * H), X, ALU.add).then_inc(a_ss, 1)
                    dve.wait_ge(a_ss, g + 1)
                    nc.vector.tensor_scalar(half, half, NORM_FLOOR, 0.5, ALU.max, ALU.mult).then_inc(a_fl, 1)
                    dve.wait_ge(a_fl, g + 1)
                    nc.vector.tensor_scalar(arn[:, u % 2].bitcast(I32), half.bitcast(I32), -0.5,
                                            float(0x5F3759DF - (1 << 22)), ALU.mult, ALU.add).then_inc(a_gs, 1)

                def normalize(u):
                    g, v = b * NU + u, u % 2
                    dve.wait_ge(a_rs, (g + 1) * RS_POOL)
                    dve.wait_ge(a_t, at("a_t", (g - 1) * 2))
                    nc.vector.tensor_tensor(heads(qnA[v], 2 * H), heads(qkA[v], 2 * H),
                                            arn[:, v].unsqueeze(2).to_broadcast([P, 2 * H, DH]), ALU.mult).then_inc(a_qn, 1)

                for u in range(0, NU, 2):
                    norms(u)
                    if u:
                        normalize(u - 1)
                    norms(u + 1)
                    normalize(u)
                normalize(NU - 1)
                for n in range(TILES + 1):
                    if n < TILES:
                        h, i = n // NU, n % 4
                        dve.wait_ge(a_s, b * TILES + (n + 1))
                        nc.vector.tensor_reduce(amx[:, i:i + 1], bank(sbank[n % 3]), X, ALU.max).then_inc(a_mx, 1)
                        dve.wait_ge(a_mx, b * TILES + (n + 1))
                        nc.vector.tensor_scalar(anm[:, i:i + 1], amx[:, i:i + 1], sc[:, h:h + 1], -1.0,
                                                ALU.mult, ALU.mult).then_inc(a_nm, 1)
                    if n >= 1:
                        m, i = n - 1, (n - 1) % 4
                        dve.wait_ge(a_e, b * TILES + (m + 1))
                        nc.vector.reciprocal(ardn[:, i:i + 1], aden[:, i:i + 1]).then_inc(a_rd, 1)
                        dve.wait_ge(a_rd, b * TILES + (m + 1))
                        nc.vector.tensor_scalar(eA[:, m % 2], eA[:, m % 2], ardn[:, i:i + 1], None, ALU.mult).then_inc(a_p, 1)
                tokens_b = tokens.rearrange("p (k d) -> p k d", k=NU)
                nc.vector.tensor_tensor(tokens_b, tokens_b, boutb[:].unsqueeze(1).to_broadcast([P, NU, DIM]),
                                        ALU.add).then_inc(a_b, 1)
                dve.wait_ge(a_b, b + 1)
                dve.wait_ge(a_o, b + 1)
                nc.vector.tensor_tensor(tokens, tokens, ps_out, ALU.add).then_inc(a_acc, 1)

            FIRST = 1

            def scale_tables(l):
                dve.wait_ge(s_wqs, (l + 1) * 16)
                nc.vector.tensor_tensor(tabl[:, 0].rearrange("p b c d -> p b (c d)"), tab[:, 0].rearrange("p b c d -> p b (c d)"),
                                        qks[:].rearrange("p c d -> p (c d)").unsqueeze(1).to_broadcast([P, NU, 2 * DH]),
                                        ALU.mult)
                for lo, hi in ((0, DH // 2), (DH // 2, 0)):
                    t = nc.vector.tensor_tensor(tabl[:, 1, :, :, lo:lo + DH // 2], tab[:, 1, :, :, lo:lo + DH // 2],
                                                qks[:, :, hi:hi + DH // 2].unsqueeze(1).to_broadcast([P, NU, 2, DH // 2]),
                                                ALU.mult)
                t.then_inc(s_tab, 1)
                dve.wait_ge(s_tab, l + 1)

            def turn(g, lb, c, last):
                has = stages(c, last)

                def odd_keys(n):
                    dve.wait_ge(l_tk, at("l_tk", g + (n + 1)))
                    nc.vector.tensor_copy(*keys(1, n % NU)).then_inc(l_kT2, 1)

                if has[1] and not has[2]:
                    odd_keys(c + 1)
                if has[2]:
                    n = c + 2
                    u = n % NU
                    for i, copied in enumerate((l_q, l_k)):
                        if i == 1 and has[1]:
                            odd_keys(c + 1)
                        half = slice(i * INNER, (i + 1) * INNER)
                        q3, t13, t23 = (heads(a[:, half], H) for a in (qk, t1, t2))
                        dve.wait_ge(copied, g + (n + 1))
                        if i == 0:
                            dve.wait_ge(l_qn, at("l_qn", g + n))
                        nc.vector.tensor_tensor(t13, q3, tabl[:, 0, u, i].unsqueeze(1).to_broadcast([P, H, DH]), ALU.mult)
                        for lo, hi in ((0, DH // 2), (DH // 2, 0)):
                            sine = nc.vector.tensor_tensor(
                                t23[:, :, lo:lo + DH // 2], q3[:, :, hi:hi + DH // 2],
                                tabl[:, 1, u, i, lo:lo + DH // 2].unsqueeze(1).to_broadcast([P, H, DH // 2]), ALU.mult)
                        sine.then_inc(l_rp, 1)
                    dve.wait_ge(l_sq, at("l_sq", g + (n + 1)))
                    nc.vector.tensor_reduce(ss[:], heads(sq[:], 2 * H), X, ALU.add).then_inc(l_ss, 1)
                    dve.wait_ge(l_ss, at("l_ss", g + (n + 1)))
                    nc.vector.tensor_scalar(ss[:], ss[:], NORM_FLOOR, 0.5, ALU.max, ALU.mult).then_inc(l_fl, 1)
                    dve.wait_ge(l_fl, g + (n + 1))
                    nc.vector.tensor_scalar(rn[:].bitcast(I32), ss[:].bitcast(I32), -0.5, float(0x5F3759DF - (1 << 22)),
                                            ALU.mult, ALU.add).then_inc(l_gs, 1)
                if has[1]:
                    n = c + 1
                    dve.wait_ge(l_s, at("l_s", g + (n + 1)))
                    nc.vector.tensor_reduce(mx[:], heads(pool0, H), X, ALU.max).then_inc(l_mx, 1)
                    dve.wait_ge(l_mx, g + (n + 1))
                    dve.wait_ge(l_p, at("l_p", g + n))
                    nc.vector.tensor_tensor(heads(es[:], H), heads(pool0, H),
                                            mx[:].unsqueeze(2).to_broadcast([P, H, KEYS]), ALU.subtract).then_inc(l_sub, 1)
                if has[1]:
                    n = c + 1
                    dve.wait_ge(l_e, g + (n + 1))
                    nc.vector.tensor_reduce(den[:], heads(es[:], H), X, ALU.add).then_inc(l_den, 1)
                    dve.wait_ge(l_den, g + (n + 1))
                    nc.vector.reciprocal(rden[:], den[:]).then_inc(l_rd, 1)
                if has[0]:
                    n = c
                    dve.wait_ge(l_o, at("l_o", g + (n + 1)))
                    xb = x[:, bass.ds((lb + n) * DIM, DIM)]
                    nc.vector.tensor_tensor(xb, xb, ps_out[:, 0:DIM], ALU.add).then_inc(l_x, 1)
                if has[2]:
                    n = c + 2
                    dve.wait_ge(l_rs, (g + (n + 1)) * RS_POOL)
                    dve.wait_ge(l_tk, at("l_tk", g + n))
                    nc.vector.tensor_tensor(heads(qn[:], 2 * H), heads(t1, 2 * H),
                                            rn[:].unsqueeze(2).to_broadcast([P, 2 * H, DH]), ALU.mult).then_inc(l_qn, 1)

            def ffn_bias(l):
                dve.wait_ge(s_wf, (l + 1) * 48)
                nc.vector.tensor_scalar(w1s[:], w1[:], sm[:, 0:1], None, ALU.mult).then_inc(f_w, 1)
                dve.wait_ge(f_b, l + 1)
                for half in range(2):
                    c0 = half * NC
                    nc.vector.tensor_tensor(b1s[:, c0:c0 + NC - 1], sm[:, 2 + c0:1 + c0 + NC], bank(1)[:, c0:c0 + NC - 1], ALU.add)
                    last = nc.vector.tensor_tensor(b1s[0:CH[-1], c0 + NC - 1:c0 + NC], sm[0:CH[-1], 1 + c0 + NC:2 + c0 + NC],
                                                   bank(1)[0:CH[-1], c0 + NC - 1:c0 + NC], ALU.add)
                last.then_inc(f_bs, 1)
                dve.wait_ge(f_bs, l + 1)

            def ffn_deviation(n):
                dve.wait_ge(f_mu, n + 1)
                dve.wait_ge(f_xn, at("f_xn", n))
                nc.vector.tensor_tensor(fd, fT, bank(1), ALU.subtract).then_inc(f_d, 1)

            def ffn_rstd(n):
                dve.wait_ge(f_var, n + 1)
                rsqrt((bank(2)[:, 0:NU], ss[:, 0:NU]), rn[:, 0:NU], rt[:, 0:NU], n + FIRST, ALU.add, EPS)
                dve.wait_ge(s_rs, (n + (FIRST + 1)) * RS)
                for k in range(NU):
                    dg = nc.vector.tensor_scalar(fdg[:, k * P:(k + 1) * P], ident, rn[:, k:k + 1], float(DIM),
                                                 ALU.mult, ALU.mult)
                dg.then_inc(f_dg, 1)

            def ffn_norm(n):
                dve.wait_ge(f_bc, n + 1)
                dve.wait_ge(f_u, at("f_u", n * NC))
                nc.vector.tensor_tensor(fxn, fd, bank(3), ALU.mult).then_inc(f_xn, 1)

            def ffn_gate(n, parity, c):
                dve.wait_ge(f_g, n * NC + (c + 1))
                if c == 0:
                    dve.wait_ge(f_o, at("f_o", n - 1))
                nc.vector.scalar_tensor_tensor(out=fh[0:CH[c], parity, c], in0=bank((4, 6, 4)[c])[0:CH[c], :],
                                               scalar=b1s[0:CH[c], c:c + 1], in1=fg[0:CH[c], c % 2],
                                               op0=ALU.add, op1=ALU.mult).then_inc(f_h, 1)

            def ffn_add(n, b):
                dve.wait_ge(f_o, at("f_o", n + 1))
                xb = x[:, bass.ds(b * SEQ, SEQ)]
                nc.vector.tensor_tensor(xb, xb, bank(6), ALU.add).then_inc(f_x, 1)

            with dve.Fori(0, L) as l:
                fold(l + 1)
                scale_tables(l)
                layer_blocks(dve, l, turn)
                n0 = l * NB
                ffn_bias(l)
                ffn_deviation(n0)
                ffn_rstd(n0)
                ffn_norm(n0)

                def ffn_turn(b, parity, first=False, last=False):
                    n = l * NB + b
                    if not last:
                        ffn_deviation(n + 1)
                    ffn_gate(n, parity, 0)
                    ffn_gate(n, parity, 1)
                    if not last:
                        ffn_rstd(n + 1)
                    ffn_gate(n, parity, 2)
                    if not last:
                        ffn_norm(n + 1)
                    if not first:
                        ffn_add(n - 1, b - 1)

                ffn_turn(0, 0, first=True)
                with dve.Fori(0, NB // 2 - 1) as pair:
                    ffn_turn(pair * 2 + 1, 1)
                    ffn_turn(pair * 2 + 2, 0)
                ffn_turn(NB - 1, 1, last=True)
                ffn_add(l * NB + (NB - 1), NB - 1)
            dve.wait_ge(f_x, at("f_x", L * NB))
            with dve.Fori(0, NB) as b:
                xb = x[:, bass.ds(b * SEQ, SEQ)]
                nc.vector.tensor_tensor(xb, xb, acc[:, bass.ds(b * SEQ, SEQ)], ALU.add).then_inc(s_fin, 1)

        @block.tensor
        def _(pe):
            def fold(n):
                pe.wait_ge(s_wa, (n + 1) * 48)
                for h in range(H):
                    rows = slice(h % 2 * DH, (h % 2 + 1) * DH)
                    to = slot(h)
                    m = nc.tensor.matmul(bank(2 + to // 4)[:, to % 4 * DIM:(to % 4 + 1) * DIM], wv[rows, h // 2], wo[rows, h // 2],
                                         start=True, stop=True)
                m.then_inc(s_m, 1)

            def project(src, i, pool):
                for s in range(2):
                    m = nc.tensor.matmul(pool[:, s * 512:(s + 1) * 512], src,
                                         wqk[:, i * INNER + s * 512:i * INNER + (s + 1) * 512], start=True, stop=True)
                return m

            def transposes(i, pool, src):
                for a in range(PAIRS):
                    t = nc.tensor.transpose(pool[:, a * P:(a + 1) * P], src[:, i * INNER + a * P:i * INNER + (a + 1) * P], ident)
                return t

            pe.wait_ge(s_ld, 16 * (4 + NB))
            pe.wait_ge(s_avg, 1)
            pe.wait_ge(s_mask, 3)
            pe.wait_ge(s_row, 2)
            fold(0)
            pe.wait_ge(s_msb, 1)

            with pe.Fori(0, NB) as b:
                pe.wait_ge(a_xn, b + 1)
                for u in range(NU):
                    t = nc.tensor.transpose(ps_x[:, u * P:(u + 1) * P], xnb[:, u * P:(u + 1) * P], ident)
                t.then_inc(a_xt, 1)
                pe.wait_ge(a_xtsb, b + 1)
                for u in range(NU + 2):
                    if u < NU:
                        g = b * NU + u
                        pe.wait_ge(a_qk, at("a_qk", g * 2))
                        project(xnT[:, u * P:(u + 1) * P], 0, pool0).then_inc(a_pj, 1)
                        project(xnT[:, u * P:(u + 1) * P], 1, pool1).then_inc(a_pj, 1)
                    if u >= 2:
                        g = b * NU + (u - 2)
                        pe.wait_ge(a_qn, at("a_qn", g + 1))
                        pe.wait_ge(a_tsb, at("a_tsb", g * 2))
                        transposes(0, pool2, qnA[u % 2]).then_inc(a_t, 1)
                        transposes(1, pool3, qnA[u % 2]).then_inc(a_t, 1)
                pe.wait_ge(a_tsb, at("a_tsb", (b + 1) * (2 * NU)))

                def scores(n):
                    h, qb = n // NU, n % NU
                    rows = slice(h % 2 * DH, (h % 2 + 1) * DH)
                    if n >= 3:
                        pe.wait_ge(a_e, b * TILES + (n - 2))
                    nc.tensor.matmul(bank(sbank[n % 3]), qTA[rows, h // 2, qb * P:(qb + 1) * P], kTA[rows, h // 2, :],
                                     start=True, stop=True).then_inc(a_s, 1)

                scores(0)
                scores(1)
                for n in range(TILES + 2 * NU + 1):
                    if n + 2 < TILES:
                        scores(n + 2)
                    if n < TILES:
                        pe.wait_ge(a_p, b * TILES + (n + 1))
                        if n >= 2:
                            pe.wait_ge(a_ptsb, b * TILES + (n - 1))
                        for k in range(NU):
                            t = nc.tensor.transpose(bank(2 + n % 2)[:, k * P:(k + 1) * P], eA[:, n % 2, k * P:(k + 1) * P], ident)
                        t.then_inc(a_pt, 1)
                    h, k = n // NU - 1, n % NU
                    if 0 <= h < H:
                        if k == 0:
                            pe.wait_ge(a_ptsb, b * TILES + n)
                        m = nc.tensor.matmul(bank(4 + h % 2), xnb[:, k * P:(k + 1) * P], pTA[:, h % 2, k, :],
                                             start=(k == 0), stop=(k == NU - 1))
                        if k == NU - 1:
                            m.then_inc(a_y, 1)
                    h, k = (n - 1) // NU - 2, (n - 1) % NU
                    if 0 <= h < H:
                        if k == 0:
                            pe.wait_ge(a_ysb, b * H + (h + 1))
                        m = nc.tensor.matmul(ps_out[:, k * DIM:(k + 1) * DIM], yA[:, h % 2 * SEQ + k * P:h % 2 * SEQ + (k + 1) * P],
                                             mh[:, slot(h)], start=(h == 0 and k == 0), stop=(h == H - 1), skip_group_check=True)
                        if h == H - 1 and k == NU - 1:
                            m.then_inc(a_o, 1)

            def turn(g, lb, c, last):
                has = stages(c, last)
                if has[2]:
                    n = c + 2
                    u = n % NU
                    block_T = xsT[:, WIN + u * P:WIN + (u + 1) * P]
                    pe.wait_ge(l_xsT, g + (n + 1))
                    pe.wait_ge(l_sub, at("l_sub", g + (n - 1)))
                    project(block_T, 0, pool0).then_inc(l_pq, 1)
                    pe.wait_ge(l_y1sb, at("l_y1sb", g + (n - 2)))
                    project(block_T, 1, pool1).then_inc(l_pk, 1)
                if has[1]:
                    n = c + 1
                    pe.wait_ge(l_qn, at("l_qn", g + (n + 1)))
                    if has[2]:
                        pe.wait_ge(l_q, g + (n + 2))
                    else:
                        pe.wait_ge(l_sub, at("l_sub", g + n))
                    transposes(0, pool0, qn[:]).then_inc(l_tq, 1)
                if has[1]:
                    n = c + 1
                    if has[2]:
                        pe.wait_ge(l_k, g + (n + 2))
                    else:
                        pe.wait_ge(l_y1sb, at("l_y1sb", g + (n - 1)))
                    transposes(1, pool1, qn[:]).then_inc(l_tk, 1)
                if has[0]:
                    n = c
                    pe.wait_ge(l_p, at("l_p", g + (n + 1)))
                    pe.wait_ge(l_y0sb, at("l_y0sb", g + n))
                    for a in range(PAIRS):
                        t = nc.tensor.transpose(pool2[:, a * P:(a + 1) * P], pn[:, a * P:(a + 1) * P], ident)
                    t.then_inc(l_pt, 1)
                if has[2]:
                    n = c + 2
                    pe.wait_ge(l_xdup, g + (n + 1))
                    for w in range(NW):
                        t = nc.tensor.transpose(ps_x[:, w * DIM:(w + 1) * DIM], xdup[:, w].rearrange("p a k -> p (a k)"), ident)
                    t.then_inc(l_xw, 1)
                if has[1]:
                    n = c + 1
                    u = n % NU
                    pe.wait_ge(l_qT, g + (n + 1))
                    pe.wait_ge(l_kT, g + (n + 1))
                    pe.wait_ge(l_kT2, g + (n + 1))
                    for s in range(2):
                        nc.tensor.matmul(pool0[:, s * 512:(s + 1) * 512], identb[:],
                                         mask[:, 0 if u == 0 else 1].rearrange("p h k -> p (h k)"), start=True, stop=False,
                                         skip_group_check=True)
                    for a in range(PAIRS):
                        for w in range(NW):
                            key0 = u * P + w * WIN
                            m = nc.tensor.matmul(pool0[w * WIN:(w + 1) * WIN, a * 2 * KEYS:(a + 1) * 2 * KEYS],
                                                 qT[:, a, w * WIN:(w + 1) * WIN], kpad[:, 2 * a:2 * a + 2, key0:key0 + KEYS],
                                                 start=False, stop=True, skip_group_check=True)
                    m.then_inc(l_s, 1)
                if has[0]:
                    n = c
                    pe.wait_ge(l_pT, g + (n + 1))
                    pe.wait_ge(l_xwsb, at("l_xwsb", g + (n + 1)))
                    windows_times(0, n, pool2).then_inc(l_y0, 1)
                if has[3]:
                    n = c + 3
                    pe.wait_ge(l_xin, g + (n + 1))
                    pe.wait_ge(l_xwsb, at("l_xwsb", g + n))
                    nc.tensor.transpose(ps_x[:, 0:P], xin[:, n % 2], ident).then_inc(l_xt, 1)
                if has[0]:
                    n = c
                    if has[1]:
                        pe.wait_ge(l_kT, g + (n + 2))
                        pe.wait_ge(l_kT2, g + (n + 2))
                    else:
                        pe.wait_ge(l_y1sb, at("l_y1sb", g + n))
                    windows_times(1, n, pool1).then_inc(l_y1, 1)
                if has[0]:
                    n = c
                    pe.wait_ge(l_y0sb, at("l_y0sb", g + (n + 1)))
                    pe.wait_ge(l_x, at("l_x", g + n))
                    for odd in range(2):
                        if odd:
                            pe.wait_ge(l_y1sb, at("l_y1sb", g + (n + 1)))
                        for h in range(odd, H, 2):
                            m = nc.tensor.matmul(ps_out[:, 0:DIM], y[:, h], mh[:, slot(h)], start=(h == 0), stop=(h == H - 1))
                    m.then_inc(l_o, 1)

            def windows_times(odd, n, pool):
                rows = slice(odd * KEYS, (odd + 1) * KEYS)
                for w in range(NW):
                    m = nc.tensor.matmul(pool[:, w * PAIRS * WIN:(w + 1) * PAIRS * WIN], xw[rows, n % NU, w],
                                         pT[rows, :, w * WIN:(w + 1) * WIN], start=True, stop=True)
                return m

            def ffn_transpose(n):
                pe.wait_ge(f_in, n + 1)
                for k in range(NU):
                    t = nc.tensor.transpose(bank(0)[:, k * P:(k + 1) * P], fin[:, k * P:(k + 1) * P], ident)
                t.then_inc(f_xt, 1)

            def ffn_mean(n):
                pe.wait_ge(f_T, n + 1)
                nc.tensor.matmul(bank(1), onesd[:], fT, start=True, stop=True).then_inc(f_mu, 1)

            def ffn_variance(n):
                pe.wait_ge(f_sq, n + 1)
                for k in range(NU):
                    m = nc.tensor.matmul(bank(2)[:, k:k + 1], fsq[:, k * P:(k + 1) * P], onesd[:, 0:1], start=True, stop=True)
                m.then_inc(f_var, 1)

            def ffn_spread(n):
                pe.wait_ge(f_dg, n + 1)
                nc.tensor.matmul(bank(3), onesd[:], fdg, start=True, stop=True).then_inc(f_bc, 1)

            def ffn_up(n, c):
                if c == 0:
                    pe.wait_ge(f_xn, at("f_xn", n + 1))
                elif c == 1:
                    pe.wait_ge(f_x, at("f_x", n - 1))
                else:
                    pe.wait_ge(f_h, at("f_h", n * NC + 1))
                for half in range(2):
                    m = nc.tensor.matmul(bank((4, 6, 4)[c] + half)[0:CH[c], :],
                                         w1s[:, half * FH + c * P:half * FH + c * P + CH[c]], fxn, start=True, stop=True)
                m.then_inc(f_u, 1)

            def ffn_down(n, parity, done):
                pe.wait_ge(f_h, at("f_h", done))
                for k in range(NU):
                    for c in range(NC):
                        rows = P if c < NC - 1 else ONES_ROW + 1
                        m = nc.tensor.matmul(bank(6)[:, k * DIM:(k + 1) * DIM], fh[0:rows, parity, c, k * P:(k + 1) * P],
                                             w2[0:rows, c], start=(c == 0), stop=(c == NC - 1))
                m.then_inc(f_o, 1)

            with pe.Fori(0, L) as l:
                fold(l + 1)
                pe.wait_ge(s_msb, l + 2)
                layer_blocks(pe, l, turn)
                pe.wait_ge(l_x, at("l_x", (l + 1) * NBLK))
                pe.wait_ge(s_wf, (l + 1) * 48)
                pe.wait_ge(f_w, l + 1)
                for half in range(2):
                    for c in range(NC):
                        col = half * NC + c
                        m = nc.tensor.matmul(bank(1)[0:CH[c], col:col + 1],
                                             w1[:, half * FH + c * P:half * FH + c * P + CH[c]], sm[:, 1:2], start=True, stop=True)
                m.then_inc(f_b, 1)
                pe.wait_ge(f_bs, l + 1)
                ffn_transpose(l * NB)
                ffn_mean(l * NB)
                ffn_transpose(l * NB + 1)
                ffn_variance(l * NB)
                ffn_spread(l * NB)

                def ffn_turn(b, parity, ahead, first=False):
                    n = l * NB + b
                    ffn_up(n, 0)
                    if ahead >= 1:
                        ffn_mean(n + 1)
                    ffn_up(n, 1)
                    if ahead >= 1:
                        ffn_variance(n + 1)
                    ffn_up(n, 2)
                    if ahead >= 2:
                        ffn_transpose(n + 2)
                    if not first:
                        ffn_down(n - 1, 1 - parity, n * NC + 2)
                    if ahead >= 1:
                        ffn_spread(n + 1)

                ffn_turn(0, 0, 2, first=True)
                with pe.Fori(0, NB // 2 - 2) as pair:
                    ffn_turn(pair * 2 + 1, 1, 2)
                    ffn_turn(pair * 2 + 2, 0, 2)
                ffn_turn(NB - 3, 1, 2)
                ffn_turn(NB - 2, 0, 1)
                ffn_turn(NB - 1, 1, 0)
                pe.wait_ge(f_x, at("f_x", l * NB + (NB - 1)))
                ffn_down(l * NB + (NB - 1), 1, (l + 1) * NB * NC)


def constants():
    q = np.arange(P)[:, None]
    key = np.arange(KEYS)[None, :]
    inside = (q % WIN <= key) & (key <= q % WIN + WIN)
    first = inside & ((q >= WIN) | (key >= WIN))
    masks = [np.where(m, 0.0, NEG) for m in (first, inside)]
    half = np.arange(0, DH, 2, dtype=np.float32)
    inv_freq = (np.float32(1.0) / np.float32(10000.0) ** (half / np.float32(DH))).astype(np.float32)
    t = np.arange(SEQ, dtype=np.float32)
    freqs = t[:, None] * inv_freq[None, :]
    freqs = np.concatenate([freqs, freqs], -1)
    base = (half + np.float32(0.4 * DH)) / np.float32(1.4 * DH)
    scale = base[None, :] ** ((t - SEQ // 2) / np.float32(WIN // 2))[:, None]
    scale = np.concatenate([scale, scale], -1)
    sign = np.where(np.arange(DH) < DH // 2, -1.0, 1.0)
    cos, sin = np.cos(freqs), np.sin(freqs) * sign
    tables = np.stack([np.stack([cos * scale, cos / scale], 1), np.stack([sin * scale, sin / scale], 1)])
    tables = tables.reshape(2, NU, P, 2, DH).transpose(2, 0, 1, 3, 4).reshape(P, -1)
    return np.ascontiguousarray(np.concatenate([np.eye(P)] + masks + [tables], 1).astype(np.float32))


def pairs_of_heads(w):
    lead = w.shape[:-2]
    n = w.shape[-1]
    w = w.reshape(*lead, PAIRS, P, n)
    return np.ascontiguousarray(np.moveaxis(w, -3, -2)).reshape(*lead, P, PAIRS * n)


def kernel(**inputs):
    import concourse.bacc as bacc
    from concourse.bass_utils import run_bass_kernel_spmd

    get = {k: np.asarray(v) for k, v in inputs.items()}
    x_in = get["L0_attn_x"]
    wqkv_a, wqkv = get["L0_attn_w_qkv"], get["L0_ffn_Wqkv"]
    L = wqkv.shape[0]
    w2 = get["L0_ffn_W2"]
    w2p = np.zeros((L, NC * P, DIM), np.float32)
    w2p[:, 0:FH] = w2
    w2p[:, (NC - 1) * P + ONES_ROW] = get["L0_ffn_b2"]
    small = np.zeros((L, P, 2 + 2 * NC), np.float32)
    small[:, :, 0] = get["L0_ffn_ln_g"]
    small[:, :, 1] = get["L0_ffn_ln_b"]
    for half in range(2):
        for c in range(NC):
            lo = half * FH + c * P
            small[:, 0:CH[c], 2 + half * NC + c] = get["L0_ffn_b1"][:, lo:lo + CH[c]]
    arrays = {
        "x_in": x_in,
        "consts": constants(),
        "a_logit": get["L0_attn_logit_scale"].reshape(H),
        "a_bout": get["L0_attn_b_out"],
        "a_wqk": wqkv_a[:, 0:2 * INNER],
        "a_wv": pairs_of_heads(wqkv_a[:, 2 * INNER:].T),
        "a_wo": pairs_of_heads(get["L0_attn_w_out"]),
        "l_wqk": wqkv[:, :, 0:2 * INNER],
        "l_wv": pairs_of_heads(wqkv[:, :, 2 * INNER:].transpose(0, 2, 1)),
        "l_wo": pairs_of_heads(get["L0_ffn_Wo"]),
        "l_scale": np.concatenate([get["L0_ffn_q_scale"], get["L0_ffn_k_scale"]], 1),
        "l_w1": get["L0_ffn_W1"],
        "l_w2": w2p.reshape(L, NC, P, DIM).transpose(0, 2, 1, 3).reshape(L, P, NC * DIM),
        "l_small": small,
    }
    arrays = {k: np.ascontiguousarray(v) for k, v in arrays.items()}
    nc = bacc.Bacc("TRN2", target_bir_lowering=False, num_devices=1)
    aps = {k: nc.dram_tensor(f"in_{k}", v.shape, F32, kind="ExternalInput").ap() for k, v in arrays.items()}
    out = nc.dram_tensor("out_0_dram", x_in.shape, F32, kind="ExternalOutput").ap()
    build(nc, out=out, **aps)
    r = run_bass_kernel_spmd(nc, [{f"in_{k}": v for k, v in arrays.items()}], core_ids=[0])
    return r.results[0]["out_0_dram"]
```
